# Optimizing a Trainium2 kernel written in Bass

```python
import numpy as np
import jax
import jax.numpy as jnp

def _softmax(x, axis=-1):
    return jax.nn.softmax(x, axis=axis)

def _gelu(x):
    return jax.nn.gelu(x, approximate=True)

def _silu(x):
    return jax.nn.silu(x)

def _sigmoid(x):
    return jax.nn.sigmoid(x)

def _layernorm(x, axis=-1, eps=1e-05):
    m = jnp.mean(x, axis=axis, keepdims=True)
    v = jnp.var(x, axis=axis, keepdims=True)
    return (x - m) / jnp.sqrt(v + eps)

def _scatter_add(tgt, idx, src, axis=0):
    return tgt.at[idx].add(src)

def _segment_sum(src, seg, n):
    return jax.ops.segment_sum(src, seg, n)
kernel_name = 'mk_adj_ffn_d2_adj_r2_fc4cd4'

def setup_inputs(seed: int=0):
    np.random.seed(seed)
    _w = jnp.asarray

    def _rec_inputs():
        import jax
        import jax.numpy as jnp
        _gk = jax.random.key(seed)
        x = -0.0005207 + 1.001 * jax.random.normal(jax.random.fold_in(_gk, 1), (8, 1024, 128), jnp.float32)
        _a = jax.random.bernoulli(jax.random.fold_in(_gk, 2), 0.00195312, (8, 1024, 1024))
        _af = _a.astype(jnp.float32)
        adj = _af
        return (x, adj)
    x, adj = _rec_inputs()

    def _L0_gnn_setup():
        import jax, jax.numpy as jnp
        import numpy as np
        NEG_BIG = -9000000000000000.0
        key = jax.random.key(seed)
        k = jax.random.split(key, 7)
        B, N, F = (16, 256, 128)
        x = jax.random.normal(k[0], (B, N, F), dtype=jnp.float32)
        adj = (jax.random.uniform(k[1], (B, N, N)) < 0.05).astype(jnp.float32)
        s = 1.0 / np.sqrt(F)
        W_w = jax.random.uniform(k[2], (F, F), minval=-s, maxval=s, dtype=jnp.float32)
        W_b = jax.random.uniform(k[3], (F,), minval=-s, maxval=s, dtype=jnp.float32)
        A = jax.random.normal(k[4], (F, F), dtype=jnp.float32) * 0.02
        s2 = 1.0 / np.sqrt(2 * F)
        gate_w = jax.random.uniform(k[5], (1, 2 * F), minval=-s2, maxval=s2, dtype=jnp.float32)
        gate_b = jax.random.uniform(k[6], (1,), minval=-s2, maxval=s2, dtype=jnp.float32)
        return {'x': x, 'adj': adj, 'W_w': W_w, 'W_b': W_b, 'A': A, 'gate_w': gate_w, 'gate_b': gate_b}
    _L0_gnn_all = _L0_gnn_setup()
    _L0_gnn_in = {k: v for k, v in _L0_gnn_all.items() if k in ('W_w', 'W_b', 'A', 'gate_w', 'gate_b')}
    del _L0_gnn_all

    def _L0_ffn_setup():
        import jax, jax.numpy as jnp
        import numpy as np
        E = 8
        K = 2
        D = 128
        H = 256
        DOUT = 128
        EPS = 1e-05
        key = jax.random.key(seed)
        ks = jax.random.split(key, 9)
        s = 0.02
        return {'x': jax.random.normal(ks[0], (4, 4096, D), jnp.float32), 'gamma': 1.0 + 0.05 * jax.random.normal(ks[1], (D,), jnp.float32), 'beta': 0.05 * jax.random.normal(ks[2], (D,), jnp.float32), 'Wr': 0.01 * jax.random.normal(ks[3], (D, E), jnp.float32), 'br': jnp.zeros((E,), jnp.float32), 'W1': s * jax.random.normal(ks[4], (E, D, H), jnp.float32), 'b1': s * jax.random.normal(ks[5], (E, H), jnp.float32), 'W2': s * jax.random.normal(ks[6], (E, H, DOUT), jnp.float32), 'b2': s * jax.random.normal(ks[7], (E, DOUT), jnp.float32)}
    _L0_ffn_all = _L0_ffn_setup()
    _L0_ffn_in = {k: v for k, v in _L0_ffn_all.items() if k in ('gamma', 'beta', 'Wr', 'br', 'W1', 'b1', 'W2', 'b2')}
    del _L0_ffn_all

    def _L1_gnn_setup():
        import jax, jax.numpy as jnp
        import numpy as np
        IN_FT = 128
        OUT_FT = 128
        key = jax.random.key(seed)
        k1, k2, k3 = jax.random.split(key, 3)
        B, N = (4, 2048)
        seq = jax.random.normal(k1, (B, N, IN_FT), dtype=jnp.float32)
        adj = jax.random.uniform(k2, (B, N, N), dtype=jnp.float32)
        limit = float(np.sqrt(6.0 / (IN_FT + OUT_FT)))
        W = jax.random.uniform(k3, (OUT_FT, IN_FT), minval=-limit, maxval=limit, dtype=jnp.float32)
        b = jnp.zeros((OUT_FT,), dtype=jnp.float32)
        alpha = jnp.array(0.25, dtype=jnp.float32)
        return {'seq': seq, 'adj': adj, 'W': W, 'b': b, 'alpha': alpha}
    _L1_gnn_all = _L1_gnn_setup()
    _L1_gnn_in = {k: v for k, v in _L1_gnn_all.items() if k in ('W', 'b', 'alpha')}
    del _L1_gnn_all

    def _L1_ffn_setup():
        import jax, jax.numpy as jnp
        import numpy as np
        TOP_K = 2
        LN_EPS = 1e-05
        key = jax.random.key(seed)
        ks = jax.random.split(key, 8)
        B, S, D, E, H = (16, 512, 128, 8, 512)
        x = jax.random.normal(ks[0], (B, S, D), dtype=jnp.float32)
        Wr = jax.random.normal(ks[1], (D, E), dtype=jnp.float32) * 0.1
        br = jnp.zeros((E,), dtype=jnp.float32)
        ln_g = jnp.ones((E, D), dtype=jnp.float32)
        ln_b = jnp.zeros((E, D), dtype=jnp.float32)
        W1 = jax.random.normal(ks[2], (E, D, H), dtype=jnp.float32) * (1.0 / np.sqrt(D))
        b1 = jnp.zeros((E, H), dtype=jnp.float32)
        W2 = jax.random.normal(ks[3], (E, H, D), dtype=jnp.float32) * (1.0 / np.sqrt(H))
        b2 = jnp.zeros((E, D), dtype=jnp.float32)
        return {'x': x, 'Wr': Wr, 'br': br, 'ln_g': ln_g, 'ln_b': ln_b, 'W1': W1, 'b1': b1, 'W2': W2, 'b2': b2}
    _L1_ffn_all = _L1_ffn_setup()
    _L1_ffn_in = {k: v for k, v in _L1_ffn_all.items() if k in ('Wr', 'br', 'ln_g', 'ln_b', 'W1', 'b1', 'W2', 'b2')}
    del _L1_ffn_all
    return {'x': x, 'adj': adj, 'L0_gnn_W_w': _L0_gnn_in['W_w'], 'L0_gnn_W_b': _L0_gnn_in['W_b'], 'L0_gnn_A': _L0_gnn_in['A'], 'L0_gnn_gate_w': _L0_gnn_in['gate_w'], 'L0_gnn_gate_b': _L0_gnn_in['gate_b'], 'L0_ffn_gamma': _L0_ffn_in['gamma'], 'L0_ffn_beta': _L0_ffn_in['beta'], 'L0_ffn_Wr': _L0_ffn_in['Wr'], 'L0_ffn_br': _L0_ffn_in['br'], 'L0_ffn_W1': _L0_ffn_in['W1'], 'L0_ffn_b1': _L0_ffn_in['b1'], 'L0_ffn_W2': _L0_ffn_in['W2'], 'L0_ffn_b2': _L0_ffn_in['b2'], 'L1_gnn_W': _L1_gnn_in['W'], 'L1_gnn_b': _L1_gnn_in['b'], 'L1_gnn_alpha': _L1_gnn_in['alpha'], 'L1_ffn_Wr': _L1_ffn_in['Wr'], 'L1_ffn_br': _L1_ffn_in['br'], 'L1_ffn_ln_g': _L1_ffn_in['ln_g'], 'L1_ffn_ln_b': _L1_ffn_in['ln_b'], 'L1_ffn_W1': _L1_ffn_in['W1'], 'L1_ffn_b1': _L1_ffn_in['b1'], 'L1_ffn_W2': _L1_ffn_in['W2'], 'L1_ffn_b2': _L1_ffn_in['b2']}

def reference(x, adj, L0_gnn_W_w, L0_gnn_W_b, L0_gnn_A, L0_gnn_gate_w, L0_gnn_gate_b, L0_ffn_gamma, L0_ffn_beta, L0_ffn_Wr, L0_ffn_br, L0_ffn_W1, L0_ffn_b1, L0_ffn_W2, L0_ffn_b2, L1_gnn_W, L1_gnn_b, L1_gnn_alpha, L1_ffn_Wr, L1_ffn_br, L1_ffn_ln_g, L1_ffn_ln_b, L1_ffn_W1, L1_ffn_b1, L1_ffn_W2, L1_ffn_b2):
    import jax
    import jax.numpy as jnp

    def _L0_gnn_ref(x, adj, W_w, W_b, A, gate_w, gate_b):
        import jax, jax.numpy as jnp
        import numpy as np
        NEG_BIG = -9000000000000000.0
        h = jnp.einsum('bnf,of->bno', x, W_w) + W_b
        hA = jnp.einsum('bjf,fg->bjg', h, A)
        e = jnp.einsum('bjl,bkl->bjk', hA, h)
        e = e + jnp.transpose(e, (0, 2, 1))
        attention = jax.nn.softmax(jnp.where(adj > 0, e, NEG_BIG), axis=1) * adj
        h_prime = jax.nn.leaky_relu(jnp.einsum('bij,bjf->bif', adj, h), negative_slope=0.2)
        g = jnp.einsum('bnf,of->bno', jnp.concatenate([x, h_prime], axis=-1), gate_w) + gate_b
        coeff = jax.nn.sigmoid(g)
        return coeff * x + (1.0 - coeff) * h_prime

    def _L0_ffn_ref(x, gamma, beta, Wr, br, W1, b1, W2, b2):
        import jax, jax.numpy as jnp
        import numpy as np
        E = 8
        K = 2
        D = 128
        H = 256
        DOUT = 128
        EPS = 1e-05
        mu = jnp.mean(x, axis=-1, keepdims=True)
        var = jnp.mean(jnp.square(x - mu), axis=-1, keepdims=True)
        xn = (x - mu) * jax.lax.rsqrt(var + EPS) * gamma + beta
        logits = jnp.einsum('bsd,de->bse', xn, Wr) + br
        top_vals, top_idx = jax.lax.top_k(logits, K)
        w = jax.nn.softmax(top_vals, axis=-1)
        w_full = jnp.einsum('bsk,bske->bse', w, jax.nn.one_hot(top_idx, E, dtype=w.dtype))
        y = jnp.zeros(x.shape[:-1] + (DOUT,), x.dtype)
        for e in range(E):
            h = jax.nn.gelu(jnp.einsum('bsd,dh->bsh', xn, W1[e]) + b1[e], approximate=False)
            y_e = jnp.einsum('bsh,hd->bsd', h, W2[e]) + b2[e]
            y = y + y_e * w_full[..., e, None]
        return y

    def _L1_gnn_ref(seq, adj, W, b, alpha):
        import jax, jax.numpy as jnp
        import numpy as np
        IN_FT = 128
        OUT_FT = 128
        h = jnp.einsum('bni,oi->bno', seq, W) + b
        h = jnp.einsum('bnm,bmo->bno', adj, h)
        return jnp.where(h > 0, h, alpha * h)

    def _L1_ffn_ref(x, Wr, br, ln_g, ln_b, W1, b1, W2, b2):
        import jax, jax.numpy as jnp
        import numpy as np
        TOP_K = 2
        LN_EPS = 1e-05
        B, S, D = x.shape
        N = B * S
        xt = x.reshape(N, D)
        logits = xt @ Wr + br
        probs = jax.nn.softmax(logits, axis=-1)
        top_p, top_idx = jax.lax.top_k(probs, TOP_K)
        weights = top_p / top_p.sum(axis=-1, keepdims=True)
        mu = xt.mean(axis=-1, keepdims=True)
        var = ((xt - mu) ** 2).mean(axis=-1, keepdims=True)
        xn = (xt - mu) * jax.lax.rsqrt(var + LN_EPS)
        xe = xn[None, :, :] * ln_g[:, None, :] + ln_b[:, None, :]
        h = jax.nn.gelu(jnp.einsum('end,edh->enh', xe, W1) + b1[:, None, :], approximate=False)
        y = jnp.einsum('enh,ehd->end', h, W2) + b2[:, None, :]
        y_tok = jnp.transpose(y, (1, 0, 2))
        sel = jnp.take_along_axis(y_tok, top_idx[:, :, None], axis=1)
        out = (weights[:, :, None] * sel).sum(axis=1)
        return out.reshape(B, S, D)
    x = x + _L0_gnn_ref(_layernorm(x, axis=-1), adj, L0_gnn_W_w, L0_gnn_W_b, L0_gnn_A, L0_gnn_gate_w, L0_gnn_gate_b)
    x = x + _L0_ffn_ref(_layernorm(x, axis=-1), L0_ffn_gamma, L0_ffn_beta, L0_ffn_Wr, L0_ffn_br, L0_ffn_W1, L0_ffn_b1, L0_ffn_W2, L0_ffn_b2)
    x = x + _L1_gnn_ref(_layernorm(x, axis=-1), adj, L1_gnn_W, L1_gnn_b, L1_gnn_alpha)
    x = x + _L1_ffn_ref(_layernorm(x, axis=-1), L1_ffn_Wr, L1_ffn_br, L1_ffn_ln_g, L1_ffn_ln_b, L1_ffn_W1, L1_ffn_b1, L1_ffn_W2, L1_ffn_b2)
    return x

_drawn_inputs = setup_inputs


def setup_inputs(seed=0):
    import zlib

    import numpy as np

    out = dict(_drawn_inputs(seed))
    spreads = {'L0_ffn_br': (0.0, 0.1),
     'L1_gnn_b': (0.0, 0.1),
     'L1_ffn_br': (0.0, 0.1),
     'L1_ffn_ln_g': (1.0, 0.2),
     'L1_ffn_ln_b': (0.0, 0.329),
     'L1_ffn_b1': (0.0, 0.323),
     'L1_ffn_b2': (0.0, 0.1)}
    factors = {'L0_ffn_gamma': 8.0,
     'L0_ffn_beta': 8.0,
     'L0_ffn_Wr': 3.066,
     'L0_ffn_b1': 8.0,
     'L0_ffn_b2': 2.909}
    for name, (base, spread) in spreads.items():
        noise = np.random.default_rng([zlib.crc32(name.encode()), seed]).standard_normal(out[name].shape)
        drawn = base * np.exp(spread * noise) if base else spread * noise
        out[name] = jnp.asarray(drawn.astype(out[name].dtype))
    for name, factor in factors.items():
        out[name] = (out[name] * factor).astype(out[name].dtype)
    return out
```

```python
import concourse.bass as bass
from concourse import mybir
from contextlib import ExitStack
import numpy as np

P = 128
D = 128
NB = 8
T = 8
NODES = P * T
NTOK = NB * NODES
E = 8
TOPK = 2
HID = (256, 512)
CH = tuple(h // P for h in HID)
EPS = 1e-5
BIG = 3.0e38

TILE = 256
HALVES = TILE // P
NTILES = -(-((NTOK * TOPK + E * (TILE - 1)) // TILE) // 8) * 8
REGION = NTOK + TILE
SPARE = E * REGION
ZROWS = SPARE + (NTILES - NTOK * TOPK // TILE) * TILE
ROW = D + 2
NSPARE = (ZROWS - SPARE) // TILE
PADS = E + NSPARE
YROWS = NTOK * TOPK + PADS * TILE
WSCALE = 64.0

_WIDTHS = [
    ("wt0", D + 1), ("ident_gate", D + 1), ("bias0", D + 1), ("wt1", D), ("bias1", D),
    ("wr0", E), ("br0", E), ("gamma", 1), ("beta", 1), ("wr1", E), ("br1", E), ("lng", E), ("lnb", E),
    ("b1_0", E * CH[0]), ("b2_0", E), ("b1_1", E * CH[1]), ("b2_1", E), ("alpha", 1),
    ("before", P), ("ones", P), ("rev", E), ("region", E), ("dest", T * TOPK), ("thresholds", NTOK // TILE),
    ("tile_rows", NTILES), ("tile_index", NTILES), ("pad_dest", PADS * HALVES),
]
COL, _at = {}, 0
for _n, _w in _WIDTHS:
    COL[_n] = (_at, _at + _w)
    _at += _w
NPARAM = _at

GROUPS = ((0, 3), (3, 6), (6, 8))

LN_STAT = ((T + 6, T + 8), (T + 6, T + 7))
LN_RATE = tuple(tuple(a + 4 for a in s) for s in LN_STAT)
LN_ALL = (LN_RATE[0], (LN_RATE[1][0], LN_RATE[1][1] + 2))
Y_ADDED = 2
CMB_GROUP, CMB_USED, CMB_ALL = (3, 1), (9, 3), (9 + 2 + T, 3)
R1_LOGITS, R1_GAP, R1_ALL = 1, (9, 10), (14, 15)
R2_BASE, R2_ALL = 6, 10
ZL_ALL = 4
NPREP = 9


def moe_gnn(nc, x, adj, params, w1_0, w2_0, w1_1, w2_1, out):
    f32, f16, i32, u32 = mybir.dt.float32, mybir.dt.float16, mybir.dt.int32, mybir.dt.uint32
    ALU, ACT, AX = mybir.AluOpType, mybir.ActivationFunctionType, mybir.AxisListType
    ds = bass.ds

    ctx = ExitStack()
    with ctx:
        def sb(name, shape, dt=f32):
            return ctx.enter_context(nc.sbuf_tensor(name, shape, dt))

        def sem(name):
            return ctx.enter_context(nc.semaphore(name))

        zq = [nc.dram_tensor(f"zq{l}", [ZROWS, ROW], f32).ap() for l in range(2)]
        yq = [nc.dram_tensor(f"yq{l}", [YROWS, D], f32).ap() for l in range(2)]
        xs = [nc.dram_tensor(f"xs{l}", [NTOK, D], f32).ap() for l in range(2)]
        tok = lambda a: a.rearrange("(q t) d -> q t d", t=T)
        x_v, out_v, xs_v = tok(x), tok(out), [tok(a) for a in xs]
        yq_v = [a[0:NTOK * TOPK, :].rearrange("(q t k) d -> q t k d", t=T, k=TOPK) for a in yq]
        w1_d, w2_d = (w1_0, w1_1), (w2_0, w2_1)

        par = sb("params", [P, NPARAM])
        col = lambda name: par[:, COL[name][0]:COL[name][1]]
        tri16, ones16 = sb("tri16", [P, P], f16), sb("ones16", [P, P], f16)
        gwr, br0f, beta_b = sb("gwr", [P, E]), sb("br0f", [P, E]), sb("beta_b", [P, P])
        g64, nalpha = sb("g64", [P, 2, E]), sb("nalpha", [P, 1])
        b1tab = [sb(f"b1tab{l}", [P, E * CH[l]]) for l in range(2)]
        w1q = [sb(f"w1q{l}", [P, E, 2, HID[l]], f16) for l in range(2)]
        w2q = [sb(f"w2q{l}", [P, E, 2, HID[l]], f16) for l in range(2)]
        ident16 = sb("ident16", [P, P], f16)
        tab = sb("tab", [P, 2, NTILES], i32)
        padtab = sb("padtab", [P, E], i32)
        tick = sb("tick", [P, 3])
        base, tid = sb("base", [P, E]), sb("tid", [P, T * TOPK])

        xin = [sb(f"xin{i}", [P, T, D]) for i in range(2)]
        yin = sb("yin", [P, T, TOPK, D])
        adjs = [sb(f"adj{i}", [P, T, NODES]) for i in range(2)]
        n1 = [sb(f"n1_{i}", [P, T, D]) for i in range(2)]
        n1T, hT = sb("n1T", [P, NODES]), sb("hT", [P, NODES])
        h = [sb(f"h{i}", [P, T, D + 1]) for i in range(2)]
        hpc = sb("hpc", [P, 2, 512])
        dif = sb("dif", [P, T, D])
        x3 = [sb(f"x3_{i}", [P, T, D]) for i in range(2)]
        z, zT = sb("z", [P, T, D]), sb("zT", [P, NODES])
        zrow = [sb(f"zrow{i}", [P, T, TOPK, ROW]) for i in range(2)]
        zrow16 = [a[:, :, :, :].bitcast(f16) for a in zrow]
        zrowu = [a[:, :, :, :].bitcast(u32) for a in zrow]
        idx = [sb(f"idx{i}", [P, T, TOPK], u32) for i in range(2)]

        st = [sb(f"st{i}", [P, T, 6]) for i in range(2)]
        mv = [sb(f"mv{i}", [P, 3, T]) for i in range(2)]
        ln_v = [sb(f"ln_v{i}", [P, 2, T]) for i in range(2)]
        ln_y = [sb(f"ln_y{i}", [P, 2, T]) for i in range(2)]
        ln_t = [sb(f"ln_t{i}", [P, 2, T]) for i in range(2)]
        ln_l = [sb(f"ln_l{i}", [P, 2, T]) for i in range(2)]
        ln_r = [sb(f"ln_r{i}", [P, 2, T]) for i in range(2)]
        ln_m = [sb(f"ln_m{i}", [P, T]) for i in range(2)]
        zs = sb("zs", [P, T])
        gl, ge, gc = sb("gl", [P, T]), sb("ge", [P, T]), sb("gc", [P, T])
        lg, eq, oh1, oh2, cand = (sb(n, [P, T, E]) for n in ("lg", "eq", "oh1", "oh2", "cand"))
        m1, m2, c1, rt_d, rt_e, rt_w = (sb(n, [P, T]) for n in ("m1", "m2", "c1", "rt_d", "rt_e", "rt_w"))
        M = sb("M", [P, T + 1, E], f16)
        pos, pp = sb("pos", [P, T, E]), sb("pp", [P, TOPK, T, E])

        alias = lambda buf, a, b: buf[:, :, :].rearrange("p a b -> p (a b)")[:, a:b]
        yflat = yin[:, :, :, :].rearrange("p a b c -> p (a b c)")
        zplace = [yflat[:, i * HALVES * ROW:(i + 1) * HALVES * ROW] for i in range(7)] + [alias(xin[1], 0, HALVES * ROW)]
        zr = [a.rearrange("p (s f) -> p s f", s=HALVES) for a in zplace]
        ye = [alias(xin[0], i * HALVES * D, (i + 1) * HALVES * D).rearrange("p (s f) -> p s f", s=HALVES) for i in range(4)]
        wst = [alias(z, 0, 1024).rearrange("p (k n) -> p k n", k=2), zT[:, :].rearrange("p (k n) -> p k n", k=2)]
        padflat = alias(adjs[1], 0, PADS * HALVES * ROW)
        padrow = padflat.rearrange("p (k s f) -> p k s f", k=PADS, s=HALVES)
        ylast = [yin[:, :, :, :],
                 adjs[0][:, 0:2, :].rearrange("p a b -> p (a b)").rearrange("p (t k d) -> p t k d", t=T, k=TOPK)]
        h32 = [alias(n1[i], 0, 1024) for i in range(2)]
        h16 = [alias(a, 0, 1024).bitcast(f16).rearrange("p (k n) -> p k n", k=2) for a in (dif, z, x3[0], x3[1])]
        zTe = [hT[:, 256 * i:256 * i + 256].bitcast(f16) for i in range(2)]
        yT = [hT[:, 512 + 256 * i:768 + 256 * i] for i in range(2)]
        le = alias(n1[0], 0, NTILES * E).rearrange("p (i e) -> p i e", e=E)
        le2 = alias(n1[1], 0, NTILES * E).rearrange("p (i e) -> p i e", e=E)
        gt = alias(dif, 0, E * (NTOK // TILE)).rearrange("p (e k) -> p e k", e=E)
        tt = hT[:, 0:4 * E].rearrange("p (k e) -> p k e", e=E)
        ti = hT[:, 512:512 + 4 * NTILES].rearrange("p (k i) -> p k i", i=NTILES)

        bank = [ctx.enter_context(nc.psum_tensor(f"bank{i}", [P, 512], f32)) for i in range(8)]
        acc, trb, hb, pb = bank[0:2], bank[2:4], bank[4:6], bank[6:8]
        zt_ps = [a[:, 0:256].bitcast(f16) for a in trb]
        hid_ps = [[bank[0], bank[1]], [bank[4], bank[5]]]
        yT_ps, y_ps = pb[0], pb[1]

        s_par, s_prep, s_prepT, s_tab, s_tabc = (
            sem(n) for n in ("s_par", "s_prep", "s_prepT", "s_tab", "s_tabc"))

        class Layer:
            def __init__(self, l):
                self.l = l
                s = lambda n: sem(f"l{l}_{n}")
                self.x_in = [s("x_in0"), s("x_in1")]
                self.adj_in = [[s(f"adj_in{i}{c}") for c in range(4)] for i in range(2)]
                self.ln, self.cmb, self.r1, self.r2, self.zl = [s("ln1"), s("ln2")], s("cmb"), s("r1"), s("r2"), s("zl")
                self.seed, self.norm = [s("seed1"), s("seed2")], [s("norm1"), s("norm2")]
                self.t1_ready, self.t1_done, self.t2_ready, self.t2_done = (
                    s("t1_ready"), s("t1_done"), s("t2_ready"), s("t2_done"))
                self.h_ready, self.h_done, self.acc_ready, self.acc_done = (
                    s("h_ready"), s("h_done"), s("acc_ready"), s("acc_done"))
                self.hT_ready, self.hp_ready, self.gate_e = s("hT_ready"), s("hp_ready"), s("gate_e")
                self.x3_stored, self.zhi = [s("x3_st0"), s("x3_st1")], s("zhi")
                self.lg_ready, self.rt_e, self.rank_ready = s("lg_ready"), s("rt_e"), s("rank_ready")
                self.scat, self.pads, self.reset = [s("scat0"), s("scat1")], s("pads"), s("reset")
                self.spare, self.pad_built = s("spare"), s("pad_built")
                self.w_in, self.w_hi, self.w_lo = [s("w_in0"), s("w_in1")], s("w_hi"), s("w_lo")
                self.b1_ps, self.b1_done = s("b1_ps"), s("b1_done")
                self.zt_ready, self.zt_done, self.hps, self.gelu = s("zt_ready"), s("zt_done"), s("hps"), s("gelu")
                self.hhi, self.h16 = s("hhi"), s("h16")
                self.yT_ps, self.yT_done, self.y_ps, self.y_done = s("yT_ps"), s("yT_done"), s("y_ps"), s("y_done")

        LY = [Layer(0), Layer(1)]
        zr_in, y_st = [sem(f"zr_in{i}") for i in range(8)], [sem(f"y_st{i}") for i in range(8)]
        ROUNDS = NTILES // 8
        f_in, f_sum, f_out = [sem("f_in0"), sem("f_in1")], sem("f_sum"), [sem("f_out0"), sem("f_out1")]
        f_add, s_tick = sem("f_add"), sem("s_tick")

        class Steps:
            def __init__(self, eng, s, per_call):
                self.eng, self.s, self.per = eng, s, per_call

            def begin(self, call):
                self.first, self.k = call * self.per, 0

            def put(self, ins):
                ins.then_inc(self.s, 1)
                self.k += 1

            def sync(self):
                self.eng.wait_ge(self.s, self.first + self.k)

            def link(self, ins):
                self.put(ins)
                self.sync()

            def end(self):
                assert self.k == self.per, (self.k, self.per)

        def batches(eng, step):
            step(0, 0, 0, 0)
            step(1, 0, 1, 1)
            with eng.Fori(1, NB // 2 - 1) as u:
                step(2 * u, u, 0, 2)
                step(2 * u + 1, u, 1, 3)
            step(NB - 2, NB // 2 - 1, 0, NB - 2)
            step(NB - 1, NB // 2 - 1, 1, NB - 1)

        def tiles(eng, step, expert=None):
            def run(first, u, least):
                e = []
                if expert is not None:
                    e = [expert(first - 1), expert(first - 2)] if least else [None, None]
                for j in range(8):
                    if expert is not None:
                        e = [expert(first + j)] + e[0:2]
                    step(first + j, u, j, least + j, e)
                return e
            run(0, 0, 0)
            with eng.Fori(1, NTILES // 8 - 1) as u:
                run(8 * u, u, 8)
            return run(NTILES - 8, NTILES // 8 - 1, NTILES - 8)

        block = ctx.enter_context(nc.Block())

        @block.sync
        def _(sp):
            sp.dma_start(par[:, :], params).then_inc(s_par, 16)

            def load_x(l, b, u, j, least):
                y = LY[l]
                if least >= 2:
                    sp.wait_ge(y.cmb, CMB_ALL[l] * (b - 2) + CMB_USED[l])
                src = x_v if l == 0 else xs_v[0]
                sp.dma_start(xin[j][:, :, :], src[ds(b * P, P), :, :]).then_inc(y.x_in[j], 16)
                if l == 1:
                    if least >= 1:
                        sp.wait_ge(y.ln[0], LN_ALL[0][1] * (b - 1) + Y_ADDED)
                    sp.dma_start(yin[:, :, :, :], yq_v[0][ds(b * P, P), :, :, :]).then_inc(y.x_in[j], 16)

            def load_adj(l, b, u, j, least):
                y = LY[l]
                if least >= 2:
                    sp.wait_ge(y.acc_ready, 2 * b - 2)
                elif l == 1:
                    sp.wait_ge(LY[0].acc_ready, 2 * NB)
                for c in range(4):
                    sp.dma_start(adjs[j][:, 2 * c:2 * c + 2, :],
                                 adj[ds(b * T + 2 * c, 2), :, :].rearrange("t p i -> p t i")).then_inc(y.adj_in[j][c], 16)

            def store_x3(l, b, u, j, least):
                sp.wait_ge(LY[l].cmb, CMB_ALL[l] * (b + 1))
                sp.dma_start(xs_v[l][ds(b * P, P), :, :], x3[j][:, :, :]).then_inc(LY[l].x3_stored[j], 16)

            def graph(l):
                if l == 1:
                    for s in y_st:
                        sp.wait_ge(s, 32 * ROUNDS)
                    for s in LY[0].x3_stored:
                        sp.wait_ge(s, 16 * (NB // 2))
                for b in range(2):
                    load_x(l, b, 0, b, b)
                    if l == 0:
                        load_adj(l, b, 0, b, b)

                def step(b, u, j, least):
                    if least < NB - 2:
                        load_adj(l, b + 2, u + 1, j, least + 2)
                        load_x(l, b + 2, u + 1, j, least + 2)
                    store_x3(l, b, u, j, least)
                batches(sp, step)

            def experts(l):
                y = LY[l]
                sp.wait_ge(s_tab, 3 * (l + 1))
                sp.wait_ge(y.pad_built, 2)
                for e in range(E):
                    first = sp.value_load(padtab[0:1, e:e + 1], min_val=e * REGION, max_val=e * REGION + NTOK)
                    sp.dma_start(zq[l][ds(first, TILE), :].rearrange("(s p) f -> p s f", p=P),
                                 padrow[:, e, :, :]).then_inc(y.pads, 16)
                for k in range(NSPARE):
                    sp.dma_start(zq[l][SPARE + k * TILE:SPARE + (k + 1) * TILE, :].rearrange("(s p) f -> p s f", p=P),
                                 padrow[:, E + k, :, :]).then_inc(y.spare, 16)
                sp.wait_ge(y.pads, 16 * E)
                for s in y.scat:
                    sp.wait_ge(s, 16 * TOPK * T * (NB // 2))

                for s in y.x3_stored:
                    sp.wait_ge(s, 16 * (NB // 2))

                def step(i, u, j, least, e):
                    row = sp.value_load(tab[0:1, 1, ds(i, 1)], min_val=0, max_val=ZROWS - TILE)
                    if least >= 8:
                        sp.wait_ge(y_st[j], 32 * (ROUNDS * l + u))
                    if least == NTILES - NSPARE:
                        sp.wait_ge(y.spare, 16 * NSPARE)
                    sp.dma_start(zr[j][:, :, :], zq[l][ds(row, TILE), :].rearrange("(s p) f -> p s f", p=P))\
                        .then_inc(zr_in[j], 16)
                    if l == 0 and least in (6, 7):
                        if least == 6:
                            sp.wait_ge(y.spare, 16 * NSPARE)
                        load_adj(1, least - 6, 0, least - 6, least - 6)
                assert NSPARE <= 8
                tiles(sp, step)

            graph(0)
            experts(0)
            graph(1)
            experts(1)

            for s in y_st:
                sp.wait_ge(s, 32 * 2 * ROUNDS)
            for s in LY[1].x3_stored:
                sp.wait_ge(s, 16 * (NB // 2))

            def load_last(b, j):
                sp.dma_start(xin[j][:, :, :], xs_v[1][b * P:(b + 1) * P, :, :]).then_inc(f_in[j], 16)
                sp.dma_start(ylast[j], yq_v[1][b * P:(b + 1) * P, :, :, :]).then_inc(f_in[j], 16)
            load_last(0, 0)
            load_last(1, 1)
            for b in range(NB):
                j = b % 2
                sp.wait_ge(f_sum, b + 1)
                sp.dma_start(out_v[b * P:(b + 1) * P, :, :], xin[j][:, :, :]).then_inc(f_out[j], 16)
                if b + 2 < NB:
                    sp.wait_ge(f_out[j], 16 * (b // 2 + 1))
                    load_last(b + 2, j)
            for s in f_out:
                sp.wait_ge(s, 16 * (NB // 2))

        @block.scalar
        def _(act):
            def seeds(y, i, call, n, least):
                act.wait_ge(y.ln[i], LN_ALL[i][y.l] * call + LN_STAT[i][y.l])
                act.activation(ln_l[i][:, 0:n, :], ln_v[i][:, 0:n, :], ACT.Ln).then_inc(y.seed[i], 1)
                act.wait_ge(y.seed[i], 2 * call + 1)
                act.activation(ln_y[i][:, 0:n, :], ln_l[i][:, 0:n, :], ACT.Exp, scale=-0.5).then_inc(y.seed[i], 1)

            def normalise(y, i, call, dst, src):
                act.wait_ge(y.ln[i], LN_ALL[i][y.l] * call + LN_RATE[i][y.l])
                for t in range(T):
                    ins = act.activation(dst[:, t, :], src[:, t, :], ACT.Identity,
                                         bias=ln_m[i][:, t:t + 1], scale=ln_r[i][:, 0, t:t + 1])
                ins.then_inc(y.norm[i], 1)

            def ln1(l, n, j, least):
                y = LY[l]
                seeds(y, 0, n, 1, least)
                if least >= 2:
                    act.wait_ge(y.cmb, CMB_ALL[l] * (n - 2) + CMB_USED[l])
                normalise(y, 0, n, n1[j], xin[j])

            def t1_evac(l, n, least, hf):
                y = LY[l]
                if least >= 1 and hf == 0:
                    act.wait_ge(y.h_ready, 3 * n)
                act.wait_ge(y.t1_ready, 2 * n + hf + 1)
                act.activation(n1T[:, 512 * hf:512 * hf + 512], trb[hf][:, :], ACT.Copy).then_inc(y.t1_done, 1)

            def t2_evac(l, n, least, hf):
                y = LY[l]
                if least >= 1 and hf == 0:
                    act.wait_ge(y.lg_ready, n)
                act.wait_ge(y.t2_ready, 2 * n + hf + 1)
                act.activation(zT[:, 512 * hf:512 * hf + 512], trb[hf][:, :], ACT.Copy).then_inc(y.t2_done, 1)

            def acc_evac(l, b, least, hf):
                y = LY[l]
                act.wait_ge(y.acc_ready, 2 * b + hf + 1)
                if not (least == 0 and hf == 0):
                    act.wait_ge(y.hT_ready, 2 * b + hf)
                if l == 0:
                    act.activation(hpc[:, 0, :], acc[hf][:, :], ACT.Copy).then_inc(y.acc_done, 1)
                else:
                    act.activation(hpc[:, 0, :], acc[hf][:, :], ACT.Relu)
                    act.activation(hpc[:, 1, :], acc[hf][:, :], ACT.Relu, scale=-1.0).then_inc(y.acc_done, 1)

            def routing_exp(l, n):
                y = LY[l]
                act.wait_ge(y.r1, R1_ALL[l] * n + R1_GAP[l])
                act.activation(rt_e[:, :], rt_d[:, :], ACT.Exp).then_inc(y.rt_e, 1)

            def load_weights(l, e):
                j = e % 2
                act.dma_start(wst[j][:, 0, 0:HID[l]], w1_d[l][e]).then_inc(LY[l].w_in[j], 16)
                act.dma_start(wst[j][:, 1, 0:HID[l]], w2_d[l][e]).then_inc(LY[l].w_in[j], 16)

            def graph(l):
                y = LY[l]
                ln1(l, 0, 0, 0)
                ln1(l, 1, 1, 1)
                for hf in range(2):
                    t1_evac(l, 0, 0, hf)
                load_weights(l, 0)
                load_weights(l, 1)
                for e in range(E):
                    j = e % 2
                    act.wait_ge(y.w_in[j], 32 * (e // 2 + 1))
                    act.activation(w1q[l][:, e, 0, :], wst[j][:, 0, 0:HID[l]], ACT.Copy,
                                   scale=g64[:, l, e:e + 1]).then_inc(y.w_hi, 1)
                    act.activation(w2q[l][:, e, 0, :], wst[j][:, 1, 0:HID[l]], ACT.Copy,
                                   scale=WSCALE).then_inc(y.w_hi, 1)
                    if e + 2 < E:
                        act.wait_ge(y.w_hi, 2 * (e + 1))
                        act.wait_ge(y.w_lo, 2 * (e + 1))
                        act.wait_ge(y.b1_ps, e + 1)
                        load_weights(l, e + 2)

                def step(b, u, j, least):
                    acc_evac(l, b, least, 0)
                    if least < NB - 1:
                        for hf in range(2):
                            t1_evac(l, b + 1, least + 1, hf)
                    acc_evac(l, b, least, 1)
                    if least >= 1:
                        for hf in range(2):
                            t2_evac(l, b - 1, least - 1, hf)
                        routing_exp(l, b - 1)
                    if l == 0:
                        act.wait_ge(y.cmb, CMB_ALL[0] * b + CMB_USED[0])
                        act.activation(ge[:, :], gl[:, :], ACT.Exp, scale=-1.0).then_inc(y.gate_e, 1)
                    seeds(y, 1, b, 1 + l, least)
                    normalise(y, 1, b, z, x3[j])
                    act.wait_ge(y.norm[1], b + 1)
                    if least >= 2:
                        act.wait_ge(y.scat[j], 16 * TOPK * T * u)
                    act.activation(zrow16[j][:, :, 0, 0:D], z[:, :, :], ACT.Copy).then_inc(y.zhi, 1)
                    if least < NB - 2:
                        ln1(l, b + 2, j, least + 2)
                batches(act, step)
                for hf in range(2):
                    t2_evac(l, NB - 1, NB - 1, hf)
                routing_exp(l, NB - 1)

            def experts(l):
                y = LY[l]
                act.wait_ge(s_tab, 3 * (l + 1))

                def expert(i):
                    return act.value_load(tab[0:1, 0, ds(i, 1)], min_val=0, max_val=E - 1)

                def gelu(i, e, least):
                    k = least % 2
                    if least >= 2:
                        act.wait_ge(y.h16, i - 1)
                    for c in range(CH[l]):
                        if c % 2 == 0:
                            act.wait_ge(y.hps, CH[l] // 2 * i + c // 2 + 1)
                        ins = act.activation(h32[k][:, 256 * c:256 * c + 256],
                                             hid_ps[k][c // 2][:, 256 * (c % 2):256 * (c % 2) + 256], ACT.Gelu,
                                             bias=b1tab[l][:, ds(e * CH[l] + c, 1)], scale=1.0 / WSCALE)
                        if c % 2 == 1:
                            ins.then_inc(y.gelu, 1)

                def yt(i, e, least):
                    act.wait_ge(y.yT_ps, i + 1)
                    act.activation(yT[least % 2], yT_ps[:, 0:TILE], ACT.Identity,
                                   bias=col(f"b2_{l}")[:, ds(e, 1)], scale=1.0 / WSCALE).then_inc(y.yT_done, 1)

                def step(i, u, j, least, e):
                    gelu(i, e[0], least)
                    if least >= 2:
                        yt(i - 2, e[2], least - 2)
                e = tiles(act, step, expert)
                yt(NTILES - 2, e[1], NTILES - 2)
                yt(NTILES - 1, e[0], NTILES - 1)

            act.wait_ge(s_par, 16)
            act.wait_ge(s_prep, NPREP)
            for l in range(2):
                graph(l)
                experts(l)

        @block.tensor
        def _(pe):
            ident = col("ident_gate")[:, 0:P]

            def t1(l, n, least):
                y, j = LY[l], least % 2
                pe.wait_ge(y.norm[0], n + 1)
                for hf in range(2):
                    if least >= 1:
                        pe.wait_ge(y.t1_done, 2 * n - 1 + hf)
                    if least >= 3:
                        pe.wait_ge(y.t2_done, 2 * (n - 3) + hf + 1)
                    for t in range(4):
                        ins = pe.transpose(trb[hf][:, t * P:t * P + P], n1[j][:, 4 * hf + t, :], ident)
                    ins.then_inc(y.t1_ready, 1)

            def h_rows(l, n, least):
                y = LY[l]
                w = col(f"wt{l}")
                for g, (a, b) in enumerate(GROUPS):
                    pe.wait_ge(y.t1_done, 2 * n + (1 if g == 0 else 2))
                    if least >= 1 or g == 2:
                        pe.wait_ge(y.h_done, 3 * n + (g == 2))
                    if least >= 3 and g == 0:
                        pe.wait_ge(y.r2, R2_ALL * (n - 3) + R2_BASE)
                    if least >= 3 and g == 1:
                        pe.wait_ge(y.r1, R1_ALL[l] * (n - 3) + R1_LOGITS)
                    for t in range(a, b):
                        ins = pe.matmul(hb[g % 2][:, (t - a) * (D + 1):(t - a) * (D + 1) + w.shape[1]],
                                        n1T[:, t * P:t * P + P], w, start=True, stop=True)
                    ins.then_inc(y.h_ready, 1)

            def aggregate(l, b, u, least, hf):
                y, j = LY[l], least % 2
                if hf == 0:
                    pe.wait_ge(y.h_done, 3 * b + 3)
                if not (least == 0 and hf == 0):
                    pe.wait_ge(y.acc_done, 2 * b - 1 + hf)
                for t in range(T):
                    if t % 2 == 0 and hf == 0:
                        pe.wait_ge(y.adj_in[j][t // 2], 16 * u + 16)
                    ins = pe.matmul(acc[hf][:, :], h[j][:, t, 0:D], adjs[j][:, t, 512 * hf:512 * hf + 512],
                                    start=(t == 0), stop=(t == T - 1))
                ins.then_inc(y.acc_ready, 1)

            def hp_rows(l, b, least):
                y = LY[l]
                for g, (a, c) in enumerate(GROUPS):
                    if least >= 1 and g == 0:
                        pe.wait_ge(y.cmb, CMB_ALL[l] * (b - 1) + CMB_USED[l])
                    if g == 2:
                        pe.wait_ge(y.cmb, CMB_ALL[l] * b + CMB_GROUP[l])
                    pe.wait_ge(y.hT_ready, 2 * b + (1 if g == 0 else 2))
                    for t in range(a, c):
                        o = (t - a) * (D + 1) if l == 0 else (t - a) * D
                        if l == 0:
                            ins = pe.matmul(pb[g % 2][:, o:o + D + 1], hT[:, t * P:t * P + P],
                                            col("ident_gate"), start=True, stop=True)
                        else:
                            ins = pe.transpose(pb[g % 2][:, o:o + D], hT[:, t * P:t * P + P], ident)
                    ins.then_inc(y.hp_ready, 1)

            def t2(l, n, least, last):
                y = LY[l]
                pe.wait_ge(y.norm[1], n + 1)
                for hf in range(2):
                    if not last:
                        pe.wait_ge(y.t1_done, 2 * (n + 2) + hf + 1)
                    else:
                        pe.wait_ge(y.t2_done, 2 * (n - 1) + hf + 1)
                    for t in range(4):
                        ins = pe.transpose(trb[hf][:, t * P:t * P + P], z[:, 4 * hf + t, :], ident)
                    ins.then_inc(y.t2_ready, 1)

            def logits(l, n, least, last):
                y = LY[l]
                w = gwr[:, :] if l == 0 else col("wr1")
                pe.wait_ge(y.t2_done, 2 * n + 2)
                if last:
                    pe.wait_ge(y.r1, R1_ALL[l] * (n - 1) + R1_LOGITS)
                else:
                    pe.wait_ge(y.h_done, 3 * (n + 2) + 2)
                for t in range(T):
                    ins = pe.matmul(hb[1][:, t * E:t * E + E], zT[:, t * P:t * P + P], w, start=True, stop=True)
                ins.then_inc(y.lg_ready, 1)

            def ranks(l, n, least, last):
                y = LY[l]
                pe.wait_ge(y.r1, R1_ALL[l] * (n + 1))
                if last:
                    pe.wait_ge(y.r2, R2_ALL * (n - 1) + R2_BASE)
                else:
                    pe.wait_ge(y.h_done, 3 * (n + 2) + 3)
                pe.matmul(hb[0][:, 0:(T + 1) * E], tri16[:, :], M[:, :, :], start=True, stop=False)
                for t in range(T):
                    ins = pe.matmul(hb[0][:, (t + 1) * E:(T + 1) * E], ones16[:, :],
                                    M[:, t:t + 1, :].to_broadcast([P, T - t, E]), start=False, stop=(t == T - 1))
                ins.then_inc(y.rank_ready, 1)

            def graph(l):
                y = LY[l]
                t1(l, 0, 0)
                h_rows(l, 0, 0)
                for e in range(E):
                    pe.wait_ge(y.w_in[e % 2], 32 * (e // 2 + 1))
                    beta = col("beta") if l == 0 else col("lnb")[:, e:e + 1]
                    for c in range(CH[l]):
                        k = e * CH[l] + c
                        ins = pe.matmul(pb[1][:, k:k + 1], wst[e % 2][:, 0, c * P:c * P + P], beta, start=True, stop=True)
                    ins.then_inc(y.b1_ps, 1)

                def step(b, u, j, least):
                    aggregate(l, b, u, least, 0)
                    if least < NB - 1:
                        t1(l, b + 1, least + 1)
                    aggregate(l, b, u, least, 1)
                    if least >= 1:
                        t2(l, b - 1, least - 1, least == NB - 1)
                    if least < NB - 1:
                        h_rows(l, b + 1, least + 1)
                    if least >= 1:
                        logits(l, b - 1, least - 1, least == NB - 1)
                    if least == 0:
                        pe.wait_ge(y.b1_done, 1)
                        pe.wait_ge(s_prep, NPREP + 1)
                    hp_rows(l, b, least)
                    if least >= 1:
                        ranks(l, b - 1, least - 1, least == NB - 1)
                batches(pe, step)
                t2(l, NB - 1, NB - 1, True)
                logits(l, NB - 1, NB - 1, True)
                ranks(l, NB - 1, NB - 1, True)

            def experts(l):
                y = LY[l]
                nb = CH[l] // 2
                pe.wait_ge(s_tab, 3 * (l + 1))

                def expert(i):
                    return pe.value_load(tab[0:1, 0, ds(i, 1)], min_val=0, max_val=E - 1)

                def turn(i, u, least):
                    j, k = least % 8, least % 2
                    pe.wait_ge(zr_in[j], 16 * (ROUNDS * l + u + 1))
                    rows = zr[j][:, :, :].bitcast(f16)
                    for v in range(2):
                        for s in range(HALVES):
                            ins = pe.transpose(zt_ps[k][:, (2 * v + s) * P:(2 * v + s + 1) * P],
                                               rows[:, s, v * D:v * D + D], ident16[:, :])
                    ins.then_inc(y.zt_ready, 1)

                def up(i, e, least):
                    k = least % 2
                    pe.wait_ge(y.zt_done, i + 1)
                    if least >= 2:
                        pe.wait_ge(y.gelu, nb * (i - 1))
                    for c in range(CH[l]):
                        o = hid_ps[k][c // 2][:, 256 * (c % 2):256 * (c % 2) + 256]
                        for n, (w, v) in enumerate(((0, 0), (0, 1), (1, 0))):
                            ins = pe.matmul(o, w1q[l][:, ds(e, 1), w, c * P:c * P + P],
                                            zTe[k][:, 256 * v:256 * v + 256], start=(n == 0), stop=(n == 2))
                        if c % 2 == 1:
                            ins.then_inc(y.hps, 1)

                def down(i, e, least):
                    k = least % 4
                    pe.wait_ge(y.h16, i + 1)
                    for c in range(CH[l]):
                        for n, (w, v) in enumerate(((0, 0), (0, 1), (1, 0))):
                            ins = pe.matmul(yT_ps[:, 0:TILE], w2q[l][:, ds(e, 1), w, c * P:c * P + P],
                                            h16[k][:, v, 256 * c:256 * c + 256],
                                            start=(c == 0 and n == 0), stop=(c == CH[l] - 1 and n == 2))
                    ins.then_inc(y.yT_ps, 1)

                def turn_back(i, least):
                    k = least % 2
                    pe.wait_ge(y.yT_done, i + 1)
                    if least >= 1:
                        pe.wait_ge(y.y_done, i)
                    for s in range(HALVES):
                        ins = pe.transpose(y_ps[:, s * P:s * P + P], yT[k][:, s * P:s * P + P], ident)
                    ins.then_inc(y.y_ps, 1)

                turn(0, 0, 0)

                def step(i, u, j, least, e):
                    if least < NTILES - 1:
                        turn(i + 1, u + (j == 7), least + 1)
                    up(i, e[0], least)
                    if least >= 3:
                        turn_back(i - 3, least - 3)
                    if least >= 2:
                        down(i - 2, e[2], least - 2)
                e = tiles(pe, step, expert)
                turn_back(NTILES - 3, NTILES - 3)
                down(NTILES - 2, e[1], NTILES - 2)
                turn_back(NTILES - 2, NTILES - 2)
                down(NTILES - 1, e[0], NTILES - 1)
                turn_back(NTILES - 1, NTILES - 1)

            pe.wait_ge(s_par, 16)
            pe.wait_ge(s_prep, NPREP)
            pe.matmul(pb[0][:, 0:E], beta_b[:, :], col("wr0"), start=True, stop=True).then_inc(s_prepT, 1)
            for l in range(2):
                graph(l)
                experts(l)

        @block.vector
        def _(dve):
            V = nc.vector
            bc = lambda a, n: a.unsqueeze(2).to_broadcast([P, a.shape[1], n])
            bt = lambda a, n: a.unsqueeze(1).to_broadcast([P, n, a.shape[1]])
            tt_ = V.tensor_tensor

            def statistics(y, i, src, steps):
                for t in range(T):
                    steps.put(V.bn_stats(st[i][:, t, :], src[:, t, :]))
                steps.sync()
                (m, q), (m_, q_) = ((st[i][:, :, a + 1], st[i][:, :, a + 2]) for a in (0, 3))
                two_mean, gap, var = (mv[i][:, a, :] for a in range(3))
                steps.put(tt_(two_mean, m, m_, ALU.add))
                steps.put(tt_(gap, m, m_, ALU.subtract))
                steps.link(tt_(var, q, q_, ALU.add))
                steps.link(tt_(gap, gap, gap, ALU.mult))
                steps.link(V.scalar_tensor_tensor(out=var, in0=gap, scalar=D / 4.0, in1=var, op0=ALU.mult, op1=ALU.add))
                if i == 0:
                    steps.put(V.tensor_scalar(ln_v[i][:, 0, :], var, 1.0 / D, EPS, ALU.mult, ALU.add))
                else:
                    steps.put(V.tensor_scalar(ln_v[i][:, 0, :], var, (1.0 + EPS) / D, EPS * EPS, ALU.mult, ALU.add))
                    if y.l == 1:
                        steps.put(V.tensor_scalar(ln_v[i][:, 1, :], var, 1.0 / D, EPS, ALU.mult, ALU.add))
                assert steps.k == LN_STAT[i][y.l]

            def inverse_root(y, i, call, least, steps):
                n = 1 + (i == 1 and y.l == 1)
                v, g, t, r = (a[i][:, 0:n, :] for a in (ln_v, ln_y, ln_t, ln_r))
                dve.wait_ge(y.seed[i], 2 * call + 2)
                steps.link(tt_(t, g, g, ALU.mult))
                steps.link(V.scalar_tensor_tensor(out=t, in0=t, scalar=-0.5, in1=v, op0=ALU.mult, op1=ALU.mult))
                if least >= 1:
                    dve.wait_ge(y.norm[i], call)
                steps.link(V.scalar_tensor_tensor(out=r, in0=t, scalar=1.5, in1=g, op0=ALU.add, op1=ALU.mult))
                steps.put(V.scalar_tensor_tensor(out=ln_m[i][:, :], in0=mv[i][:, 0, :], scalar=-0.5,
                                                 in1=ln_r[i][:, 0, :], op0=ALU.mult, op1=ALU.mult))
                assert steps.k == LN_RATE[i][y.l]
                if n == 2:
                    steps.link(tt_(zs[:, :], ln_v[i][:, 0, :], ln_r[i][:, 0, :], ALU.mult))
                    steps.put(tt_(zs[:, :], zs[:, :], ln_r[i][:, 1, :], ALU.mult))
                steps.end()

            def prepare():
                ops = [
                    V.tensor_copy(tri16[:, :], col("before")),
                    V.tensor_copy(ones16[:, :], col("ones")),
                    V.tensor_copy(ident16[:, :], col("ident_gate")[:, 0:P]),
                    V.tensor_scalar(gwr[:, :], col("wr0"), col("gamma"), None, ALU.mult),
                    V.tensor_scalar(beta_b[:, :], col("ones"), col("beta"), None, ALU.mult),
                    V.tensor_scalar(g64[:, 0, :], col("ones")[:, 0:E], col("gamma"), WSCALE, ALU.mult, ALU.mult),
                    V.tensor_scalar(g64[:, 1, :], col("lng"), WSCALE, None, ALU.mult),
                    V.tensor_scalar(nalpha[:, :], col("alpha"), -1.0, None, ALU.mult),
                    V.memset(M[:, :, :], 0.0),
                ]
                for ins in ops:
                    ins.then_inc(s_prep, 1)
                dve.wait_ge(s_prep, len(ops))
                assert len(ops) == NPREP
                dve.wait_ge(s_prepT, 1)
                tt_(br0f[:, :], pb[0][:, 0:E], col("br0"), ALU.add).then_inc(s_prep, 1)
                dve.wait_ge(s_prep, NPREP + 1)

            def graph(l):
                y = LY[l]
                ln1, ln2 = (Steps(dve, y.ln[i], LN_ALL[i][l]) for i in range(2))
                r1, r2 = Steps(dve, y.r1, R1_ALL[l]), Steps(dve, y.r2, R2_ALL)
                cmb, zl = Steps(dve, y.cmb, CMB_ALL[l]), Steps(dve, y.zl, ZL_ALL)
                W = D + 1 if l == 0 else D
                bias = col(f"bias{l}")

                def ln1_stats(n, u, j):
                    ln1.begin(n)
                    dve.wait_ge(y.x_in[j], (16 + 16 * l) * (u + 1))
                    if l == 1:
                        for k in range(TOPK):
                            ln1.link(tt_(xin[j][:, :, :], xin[j][:, :, :], yin[:, :, k, :], ALU.add))
                    statistics(y, 0, xin[j], ln1)

                def h_evac(n, least):
                    j = least % 2
                    if least >= 2:
                        dve.wait_ge(y.acc_ready, 2 * n - 2)
                    for g, (a, b) in enumerate(GROUPS):
                        dve.wait_ge(y.h_ready, 3 * n + g + 1)
                        src = hb[g % 2][:, 0:(b - a) * (D + 1)].rearrange("p (t w) -> p t w", w=D + 1)[:, :, 0:W]
                        tt_(h[j][:, a:b, 0:W], src, bt(bias, b - a), ALU.add).then_inc(y.h_done, 1)

                def hT_evac(b, hf):
                    dve.wait_ge(y.acc_done, 2 * b + hf + 1)
                    o = hT[:, 512 * hf:512 * hf + 512]
                    if l == 0:
                        ins = V.scalar_tensor_tensor(out=o, in0=hpc[:, 0, :], scalar=0.2, in1=hpc[:, 0, :],
                                                     op0=ALU.mult, op1=ALU.max)
                    else:
                        ins = V.scalar_tensor_tensor(out=o, in0=hpc[:, 1, :], scalar=nalpha[:, 0:1],
                                                     in1=hpc[:, 0, :], op0=ALU.mult, op1=ALU.add)
                    ins.then_inc(y.hT_ready, 1)

                def route_1(n):
                    r1.begin(n)
                    dve.wait_ge(y.lg_ready, n + 1)
                    ps = hb[1][:, 0:T * E].rearrange("p (t e) -> p t e", e=E)
                    if l == 0:
                        r1.link(tt_(lg[:, :, :], ps, bt(br0f[:, :], T), ALU.add))
                    else:
                        r1.link(tt_(lg[:, :, :], ps, bc(zs[:, :], E), ALU.mult))
                        r1.link(tt_(lg[:, :, :], lg[:, :, :], bt(col("br1"), T), ALU.add))

                    def choose(src, m, oh):
                        r1.link(tt_(cand[:, :, :], src[:, :, :], bc(m[:, :], E), ALU.is_equal))
                        r1.link(tt_(cand[:, :, :], cand[:, :, :], bt(col("rev"), T), ALU.mult))
                        r1.link(V.tensor_reduce(c1[:, :], cand[:, :, :], AX.X, ALU.max))
                        r1.link(tt_(oh[:, :, :], bt(col("rev"), T), bc(c1[:, :], E), ALU.is_equal))

                    r1.link(V.tensor_reduce(m1[:, :], lg[:, :, :], AX.X, ALU.max))
                    choose(lg, m1, oh1)
                    r1.link(V.scalar_tensor_tensor(out=eq[:, :, :], in0=oh1[:, :, :], scalar=-BIG,
                                                   in1=lg[:, :, :], op0=ALU.mult, op1=ALU.add))
                    r1.link(V.tensor_reduce(m2[:, :], eq[:, :, :], AX.X, ALU.max))
                    r1.put(tt_(rt_d[:, :], m2[:, :], m1[:, :], ALU.subtract))
                    assert r1.k == R1_GAP[l]
                    choose(eq, m2, oh2)
                    r1.put(tt_(M[:, 0:T, :], oh1[:, :, :], oh2[:, :, :], ALU.add))
                    r1.end()

                def route_2(n, u, j):
                    r2.begin(n)
                    w_out = zrow[j][:, :, :, D + 1]
                    dve.wait_ge(y.rt_e, n + 1)
                    r2.link(V.tensor_scalar(rt_w[:, :], rt_e[:, :], 1.0, None, ALU.add))
                    r2.link(V.reciprocal(rt_w[:, :], rt_w[:, :]))
                    r2.put(V.tensor_copy(w_out[:, :, 0], rt_w[:, :]))
                    r2.put(tt_(w_out[:, :, 1], rt_w[:, :], rt_e[:, :], ALU.mult))
                    dve.wait_ge(y.rank_ready, n + 1)
                    r2.link(tt_(pos[:, :, :], hb[0][:, 0:T * E].rearrange("p (t e) -> p t e", e=E),
                                bt(base[:, :], T), ALU.add))
                    r2.put(tt_(base[:, :], base[:, :], hb[0][:, T * E:(T + 1) * E], ALU.add))
                    assert r2.k == R2_BASE
                    r2.put(tt_(pp[:, 0, :, :], pos[:, :, :], oh1[:, :, :], ALU.mult))
                    r2.link(tt_(pp[:, 1, :, :], pos[:, :, :], oh2[:, :, :], ALU.mult))
                    for k in range(TOPK):
                        with nc.allow_low_precision(reason="whole numbers, exact in float32"):
                            r2.put(V.tensor_reduce(idx[j][:, :, k], pp[:, k, :, :], AX.X, ALU.add))
                    r2.end()

                def combine(b, u, j, least):
                    cmb.begin(b)
                    if least >= 2:
                        dve.wait_ge(y.x3_stored[j], 16 * u)
                    for g, (a, c) in enumerate(GROUPS):
                        dve.wait_ge(y.hp_ready, 3 * b + g + 1)
                        ps = pb[g % 2][:, 0:(c - a) * W].rearrange("p (t w) -> p t w", w=W)
                        if l == 0:
                            cmb.put(tt_(dif[:, a:c, :], n1[j][:, a:c, :], ps[:, :, 0:D], ALU.subtract))
                            cmb.put(tt_(x3[j][:, a:c, :], xin[j][:, a:c, :], ps[:, :, 0:D], ALU.add))
                            cmb.put(tt_(gl[:, a:c], h[j][:, a:c, D], ps[:, :, D], ALU.add))
                        else:
                            cmb.put(tt_(x3[j][:, a:c, :], xin[j][:, a:c, :], ps, ALU.add))

                def gate(b, j):
                    dve.wait_ge(y.gate_e, b + 1)
                    cmb.link(V.tensor_scalar(gc[:, :], ge[:, :], 1.0, None, ALU.add))
                    cmb.link(V.reciprocal(gc[:, :], gc[:, :]))
                    for t in range(T):
                        cmb.put(V.scalar_tensor_tensor(out=x3[j][:, t, :], in0=dif[:, t, :], scalar=gc[:, t:t + 1],
                                                       in1=x3[j][:, t, :], op0=ALU.mult, op1=ALU.add))

                def rows(b, u, j):
                    zl.begin(b)
                    dve.wait_ge(y.zhi, b + 1)
                    zl.link(tt_(zrow16[j][:, :, 0, D:2 * D], z[:, :, :], zrow16[j][:, :, 0, 0:D], ALU.subtract))
                    zl.put(V.tensor_copy(zrow16[j][:, :, 1, 0:2 * D], zrow16[j][:, :, 0, 0:2 * D]))
                    zl.link(V.tensor_copy(zrowu[j][:, :, :, D], tid[:, :].rearrange("p (t k) -> p t k", k=TOPK)))
                    zl.put(V.tensor_scalar(tid[:, :], tid[:, :], float(NODES * TOPK), None, ALU.add))
                    zl.end()

                V.tensor_copy(base[:, :], col("region")).then_inc(y.reset, 1)
                V.tensor_copy(tid[:, :], col("dest")).then_inc(y.reset, 1)
                dve.wait_ge(y.reset, 2)
                for n in range(2):
                    ln1_stats(n, 0, n)
                    inverse_root(y, 0, n, n, ln1)
                h_evac(0, 0)
                for e in range(E):
                    dve.wait_ge(y.w_in[e % 2], 32 * (e // 2 + 1))
                    dve.wait_ge(y.w_hi, 2 * (e + 1))
                    V.scalar_tensor_tensor(out=w1q[l][:, e, 1, :], in0=wst[e % 2][:, 0, 0:HID[l]],
                                           scalar=g64[:, l, e:e + 1], in1=w1q[l][:, e, 0, :],
                                           op0=ALU.mult, op1=ALU.subtract).then_inc(y.w_lo, 1)
                    V.scalar_tensor_tensor(out=w2q[l][:, e, 1, :], in0=wst[e % 2][:, 1, 0:HID[l]],
                                           scalar=WSCALE, in1=w2q[l][:, e, 0, :],
                                           op0=ALU.mult, op1=ALU.subtract).then_inc(y.w_lo, 1)
                dve.wait_ge(y.b1_ps, E)
                tt_(b1tab[l][:, :], pb[1][:, 0:E * CH[l]], col(f"b1_{l}"), ALU.add).then_inc(y.b1_done, 1)

                def step(b, u, j, least):
                    hT_evac(b, 0)
                    hT_evac(b, 1)
                    if least < NB - 1:
                        h_evac(b + 1, least + 1)
                    if least >= 1:
                        route_1(b - 1)
                    combine(b, u, j, least)
                    if least >= 1:
                        route_2(b - 1, u, 1 - j)
                    if l == 0:
                        gate(b, j)
                    cmb.sync()
                    cmb.end()
                    ln2.begin(b)
                    statistics(y, 1, x3[j], ln2)
                    inverse_root(y, 1, b, least, ln2)
                    if least < NB - 2:
                        ln1_stats(b + 2, u + 1, j)
                    rows(b, u, j)
                    if least < NB - 2:
                        inverse_root(y, 0, b + 2, least + 2, ln1)
                batches(dve, step)
                route_1(NB - 1)
                route_2(NB - 1, NB // 2 - 1, 1)

            def tables(l):
                c = Steps(dve, s_tabc, 12)
                c.begin(l)
                dve.wait_ge(LY[l].r2, R2_ALL * NB)
                n, k, upto = tt[:, 0, :], tt[:, 1, :], tt[:, 2, :]
                c.put(V.memset(tt[:, 3, :], 0.0))
                c.link(tt_(n, base[:, :], col("region"), ALU.subtract))
                c.link(tt_(gt, bc(n, NTOK // TILE), bt(col("thresholds"), E), ALU.is_gt))
                c.link(V.tensor_reduce(k, gt, AX.X, ALU.add))
                c.link(V.tensor_tensor_scan(upto, k, tt[:, 3, :], 0.0, ALU.add, ALU.add))
                c.link(tt_(le, bt(upto, NTILES), bc(col("tile_index"), E), ALU.is_le))
                c.link(V.tensor_reduce(ti[:, 0, :], le, AX.X, ALU.add))
                c.link(tt_(le2, le, bt(k, NTILES), ALU.mult))
                c.link(V.tensor_reduce(ti[:, 1, :], le2, AX.X, ALU.add))
                c.link(V.scalar_tensor_tensor(out=ti[:, 1, :], in0=ti[:, 1, :], scalar=-float(TILE),
                                              in1=col("tile_rows"), op0=ALU.mult, op1=ALU.add))
                c.link(V.scalar_tensor_tensor(out=ti[:, 1, :], in0=ti[:, 0, :], scalar=float(REGION),
                                              in1=ti[:, 1, :], op0=ALU.mult, op1=ALU.add))
                c.link(V.tensor_scalar(ti[:, 0, :], ti[:, 0, :], float(E - 1), None, ALU.min))
                c.end()
                V.tensor_copy(tab[:, 0, :], ti[:, 0, :]).then_inc(s_tab, 1)
                V.tensor_copy(tab[:, 1, :], ti[:, 1, :]).then_inc(s_tab, 1)
                V.tensor_copy(padtab[:, :], base[:, :]).then_inc(s_tab, 1)

            def experts(l):
                y = LY[l]
                nb = CH[l] // 2
                dve.wait_ge(s_tab, 3 * (l + 1))

                def z_evac(i, least):
                    k = least % 2
                    dve.wait_ge(y.zt_ready, i + 1)
                    if least >= 2:
                        dve.wait_ge(y.hps, nb * (i - 1))
                    V.tensor_copy(zTe[k], zt_ps[k]).then_inc(y.zt_done, 1)

                def split(i, least):
                    k, n = least % 2, HID[l] * TILE // P
                    o = h16[least % 4]
                    dve.wait_ge(y.gelu, nb * (i + 1))
                    V.tensor_copy(o[:, 0, 0:n], h32[k][:, 0:n]).then_inc(y.hhi, 1)
                    dve.wait_ge(y.hhi, i + 1)
                    tt_(o[:, 1, 0:n], h32[k][:, 0:n], o[:, 0, 0:n], ALU.subtract).then_inc(y.h16, 1)

                def y_evac(i, u, least):
                    j = least % 4
                    dve.wait_ge(y.y_ps, i + 1)
                    if least >= 4:
                        dve.wait_ge(y_st[(least - 4) % 8], 32 * (ROUNDS * l + u + 1))
                    for s in range(HALVES):
                        ins = V.tensor_scalar(ye[j][:, s, :], y_ps[:, s * P:s * P + P],
                                              zr[least % 8][:, s, D + 1:D + 2], None, ALU.mult)
                    ins.then_inc(y.y_done, 1)

                z_evac(0, 0)

                def step(i, u, j, least, e):
                    if least < NTILES - 1:
                        z_evac(i + 1, least + 1)
                    if least >= 1:
                        split(i - 1, least - 1)
                    if least >= 3:
                        y_evac(i - 3, u - (j < 7), least - 3)
                tiles(dve, step)
                y_evac(NTILES - 3, (NTILES - 7) // 8, NTILES - 3)
                split(NTILES - 1, NTILES - 1)
                y_evac(NTILES - 2, (NTILES - 6) // 8, NTILES - 2)
                y_evac(NTILES - 1, (NTILES - 5) // 8, NTILES - 1)

            dve.wait_ge(s_par, 16)
            prepare()
            for l in range(2):
                graph(l)
                tables(l)
                experts(l)
            for b in range(NB):
                j = b % 2
                dve.wait_ge(f_in[j], 32 * (b // 2 + 1))
                tt_(xin[j][:, :, :], xin[j][:, :, :], ylast[j][:, :, 0, :], ALU.add).then_inc(f_add, 1)
                dve.wait_ge(f_add, b + 1)
                tt_(xin[j][:, :, :], xin[j][:, :, :], ylast[j][:, :, 1, :], ALU.add).then_inc(f_sum, 1)

        @block.gpsimd
        def _(pool):
            def pass_on(call):
                pool.wait_ge(s_tick, call + 1)
                pool.tensor_tensor(tick[:, 2:3], tick[:, 0:1], tick[:, 1:2], ALU.add).then_inc(s_tick, 1)

            pool.wait_ge(s_par, 16)
            pool.memset(tick[:, :], 0.0).then_inc(s_tick, 1)
            pool.wait_ge(s_tick, 1)
            for l in range(2):
                y = LY[l]

                def send(b, u, j, least):
                    if least == NB - 1:
                        pool.wait_ge(y.acc_ready, 2 * NB)
                        pool.memset(padflat, 0.0).then_inc(y.pad_built, 1)
                        pool.wait_ge(y.pad_built, 1)
                        pool.tensor_copy(padrow[:, :, :, D].bitcast(u32),
                                         col("pad_dest").rearrange("p (k s) -> p k s", s=HALVES)).then_inc(y.pad_built, 1)
                    pool.wait_ge(y.zl, ZL_ALL * (b + 1))
                    pool.wait_ge(y.r2, R2_ALL * (b + 1))
                    pass_on(l * (NB + NTILES) + b)
                    for t in range(T):
                        for k in range(TOPK):
                            pool.indirect_dma_start(
                                out=zq[l], out_offset=bass.IndirectOffsetOnAxis(ap=idx[j][:, t, k:k + 1], axis=0),
                                in_=zrow[j][:, t, k, :], in_offset=None).then_inc(y.scat[j], 16)
                batches(pool, send)

                def give_back(i, u, j, least, e):
                    pool.wait_ge(y.y_done, i + 1)
                    pass_on(l * (NB + NTILES) + NB + i)
                    for s in range(HALVES):
                        pool.indirect_dma_start(
                            out=yq[l],
                            out_offset=bass.IndirectOffsetOnAxis(ap=zr[j][:, s, D:D + 1].bitcast(u32), axis=0),
                            in_=ye[j % 4][:, s, :], in_offset=None).then_inc(y_st[j], 16)
                tiles(pool, give_back)


def _columns(**given):
    import numpy as _np
    a = _np.zeros((P, NPARAM), _np.float32)
    for name, v in given.items():
        lo, hi = COL[name]
        a[:, lo:hi] = v
    return a


def kernel(**inputs):
    import numpy as _np
    import concourse.bacc as _bacc
    from concourse import mybir as _mybir
    from concourse.bass_utils import run_bass_kernel_spmd as _run

    g = {k: _np.asarray(v) for k, v in inputs.items()}
    row = lambda v: _np.broadcast_to(v.reshape(1, -1), (P, v.size))
    eye = _np.eye(P, dtype=_np.float32)
    p = _np.arange(P)
    gate = g["L0_gnn_gate_w"][0]
    params = _columns(
        wt0=_np.concatenate([g["L0_gnn_W_w"].T, gate[0:D, None]], axis=1),
        ident_gate=_np.concatenate([eye, gate[D:2 * D, None]], axis=1),
        bias0=row(_np.concatenate([g["L0_gnn_W_b"], g["L0_gnn_gate_b"]])),
        wt1=g["L1_gnn_W"].T, bias1=row(g["L1_gnn_b"]),
        wr0=g["L0_ffn_Wr"], br0=row(g["L0_ffn_br"]),
        gamma=g["L0_ffn_gamma"][:, None], beta=g["L0_ffn_beta"][:, None],
        wr1=g["L1_ffn_Wr"], br1=row(g["L1_ffn_br"]),
        lng=g["L1_ffn_ln_g"].T, lnb=g["L1_ffn_ln_b"].T,
        b1_0=g["L0_ffn_b1"].reshape(E * CH[0], P).T, b2_0=g["L0_ffn_b2"].T,
        b1_1=g["L1_ffn_b1"].reshape(E * CH[1], P).T, b2_1=g["L1_ffn_b2"].T,
        alpha=g["L1_gnn_alpha"].reshape(1, 1),
        before=(p[:, None] < p[None, :]), ones=1.0, rev=E - _np.arange(E), region=_np.arange(E) * REGION,
        dest=(p[:, None] * T * TOPK + _np.arange(T * TOPK)[None, :]),
        thresholds=_np.arange(NTOK // TILE) * TILE,
        tile_rows=_np.arange(NTILES) * TILE, tile_index=_np.arange(NTILES),
        pad_dest=NTOK * TOPK + _np.arange(PADS * HALVES)[None, :] * P + p[:, None],
    )
    adj = g["adj"].reshape(NB, P, T, P, T).transpose(0, 4, 3, 2, 1).reshape(NB * T, P, NODES)
    down = lambda w, l: w.reshape(E, CH[l], P, D).transpose(0, 2, 1, 3).reshape(E, P, HID[l])
    arrays = {
        "x": g["x"].reshape(NTOK, D), "adj": adj, "params": params,
        "w1_0": g["L0_ffn_W1"], "w2_0": down(g["L0_ffn_W2"], 0),
        "w1_1": g["L1_ffn_W1"], "w2_1": down(g["L1_ffn_W2"], 1),
    }
    arrays = {f"in_{k}_dram": _np.ascontiguousarray(v) for k, v in arrays.items()}

    nc = _bacc.Bacc("TRN2", target_bir_lowering=False, num_devices=1)
    args = [nc.dram_tensor(k, v.shape, _mybir.dt.from_np(v.dtype), kind="ExternalInput").ap() for k, v in arrays.items()]
    out = nc.dram_tensor("out_dram", (NTOK, D), _mybir.dt.float32, kind="ExternalOutput").ap()
    moe_gnn(nc, *args, out)
    r = _run(nc, [arrays], core_ids=[0])
    return r.results[0]["out_dram"].reshape(NB, NODES, D)
```

```python
import concourse.bass as bass
from concourse import mybir
from contextlib import ExitStack
from itertools import chain
import numpy as np

P = 128
D = 128
NB = 8
T = 8
NODES = P * T
NTOK = NB * NODES
E = 8
TOPK = 2
HID = (256, 512)
CH = tuple(h // P for h in HID)
EPS = 1e-5
BIG = 3.0e38

TILE = 256
HALVES = TILE // P
NTILES = -(-((NTOK * TOPK + E * (TILE - 1)) // TILE) // 8) * 8
REGION = NTOK + TILE
SPARE = E * REGION
ZROWS = SPARE + (NTILES - NTOK * TOPK // TILE) * TILE
ROW = D + 2
NSPARE = (ZROWS - SPARE) // TILE
PADS = E + NSPARE
YROWS = NTOK * TOPK + PADS * TILE
WSCALE = 64.0

_WIDTHS = [
    ("wt0", D + 1), ("ident_gate", D + 1), ("bias0", D + 1), ("wt1", D), ("bias1", D),
    ("wr0", E), ("br0", E), ("gamma", 1), ("beta", 1), ("wr1", E), ("br1", E), ("lng", E), ("lnb", E),
    ("b1_0", E * CH[0]), ("b2_0", E), ("b1_1", E * CH[1]), ("b2_1", E), ("alpha", 1),
    ("before", P), ("ones", P), ("rev", E), ("region", E), ("dest", T * TOPK), ("thresholds", NTOK // TILE),
    ("tile_rows", NTILES), ("tile_index", NTILES), ("pad_dest", PADS * HALVES),
]
COL, _at = {}, 0
for _n, _w in _WIDTHS:
    COL[_n] = (_at, _at + _w)
    _at += _w
NPARAM = _at

FREE = 2
GROUPS = ((0, 3), (3, 6), (6, 8))

NEWTON, ROOT_GUESS = 3, float(0x5F3759DF)
BN1_ALL = (T, T + 2)
Y_ADDED = 2
NRM_RATE = tuple(10 + 3 * NEWTON + k for k in (0, 1))
NRM_ALL = (NRM_RATE[0], NRM_RATE[1] + 2)
CMB_GROUP, CMB_USED, CMB_ALL = (3, 1), (9, 3), (9 + 2 + T, 3)
R1_LOGITS, R1_GAP, R1_ALL = 1, (9, 10), (14, 15)
R2_BASE, R2_ALL = 6, 10
ZL_ALL = 4
NPREP = 9


def moe_gnn(nc, x, adj, params, w1_0, w2_0, w1_1, w2_1, out):
    f32, f16, i32, u32 = mybir.dt.float32, mybir.dt.float16, mybir.dt.int32, mybir.dt.uint32
    ALU, ACT, AX = mybir.AluOpType, mybir.ActivationFunctionType, mybir.AxisListType
    ds = bass.ds

    ctx = ExitStack()
    with ctx:
        def sb(name, shape, dt=f32):
            return ctx.enter_context(nc.sbuf_tensor(name, shape, dt))

        def sem(name):
            return ctx.enter_context(nc.semaphore(name))

        zq = [nc.dram_tensor(f"zq{l}", [ZROWS, ROW], f32).ap() for l in range(2)]
        yq = [nc.dram_tensor(f"yq{l}", [YROWS, D], f32).ap() for l in range(2)]
        xs = [nc.dram_tensor(f"xs{l}", [NTOK, D], f32).ap() for l in range(2)]
        tok = lambda a: a.rearrange("(q t) d -> q t d", t=T)
        x_v, out_v, xs_v = tok(x), tok(out), [tok(a) for a in xs]
        yq_v = [a[0:NTOK * TOPK, :].rearrange("(q t k) d -> q t k d", t=T, k=TOPK) for a in yq]
        w1_d, w2_d = (w1_0, w1_1), (w2_0, w2_1)

        par = sb("params", [P, NPARAM])
        col = lambda name: par[:, COL[name][0]:COL[name][1]]
        tri16, ones16 = sb("tri16", [P, P], f16), sb("ones16", [P, P], f16)
        gwr, br0f, beta_b = sb("gwr", [P, E]), sb("br0f", [P, E]), sb("beta_b", [P, P])
        g64, nalpha = sb("g64", [P, 2, E]), sb("nalpha", [P, 1])
        b1tab = [sb(f"b1tab{l}", [P, E * CH[l]]) for l in range(2)]
        wmem = [sb(f"w{i}mem", [P, E * 2 * max(HID)], f16) for i in (1, 2)]
        w1q, w2q = ([m[:, 0:E * 2 * HID[l]].rearrange("p (e k n) -> p e k n", e=E, k=2) for l in range(2)] for m in wmem)
        ident16 = sb("ident16", [P, P], f16)
        tab = sb("tab", [P, 2, NTILES], i32)
        padtab = sb("padtab", [P, E], i32)
        warm = sb("warm", [P, 3])
        tick, spark = sb("tick", [P, 4]), sb("spark", [P, 4])
        base, tid = sb("base", [P, E]), sb("tid", [P, T * TOPK])

        xin = [sb(f"xin{i}", [P, T, D]) for i in range(2)]
        xc = [sb(f"xc{i}", [P, T, D]) for i in range(2)]
        yin = sb("yin", [P, T, TOPK, D])
        adjs = [sb(f"adj{i}", [P, T, NODES]) for i in range(2)]
        n1 = [sb(f"n1_{i}", [P, T, D]) for i in range(2)]
        n1T, hT = sb("n1T", [P, NODES]), sb("hT", [P, NODES])
        h = [sb(f"h{i}", [P, T, D + 1]) for i in range(2)]
        hpc = sb("hpc", [P, 2, 512])
        dif = sb("dif", [P, T, D])
        x3 = [sb(f"x3_{i}", [P, T, D]) for i in range(2)]
        z, zT = sb("z", [P, T, D]), sb("zT", [P, NODES])
        zrow = [sb(f"zrow{i}", [P, T, TOPK, ROW]) for i in range(2)]
        zrow16 = [a[:, :, :, :].bitcast(f16) for a in zrow]
        zrowu = [a[:, :, :, :].bitcast(u32) for a in zrow]
        idx = [sb(f"idx{i}", [P, T, TOPK], u32) for i in range(2)]

        st = sb("st", [P, 2, T, 6])
        mv = sb("mv", [P, 3, 2, T])
        ln_v, ln_t, ln_r = (sb(n, [P, 3, T]) for n in ("ln_v", "ln_t", "ln_r"))
        ln_m = sb("ln_m", [P, 2, T])
        zs = sb("zs", [P, T])
        gl, ge, gc = sb("gl", [P, T]), sb("ge", [P, T]), sb("gc", [P, T])
        lg, eq, oh1, oh2, cand = (sb(n, [P, T, E]) for n in ("lg", "eq", "oh1", "oh2", "cand"))
        m1, m2, c1, rt_d, rt_e, rt_w = (sb(n, [P, T]) for n in ("m1", "m2", "c1", "rt_d", "rt_e", "rt_w"))
        M = sb("M", [P, T + 1, E], f16)
        pos, pp = sb("pos", [P, T, E]), sb("pp", [P, TOPK, T, E])

        alias = lambda buf, a, b: buf[:, :, :].rearrange("p a b -> p (a b)")[:, a:b]
        yflat = yin[:, :, :, :].rearrange("p a b c -> p (a b c)")
        zplace = [yflat[:, i * HALVES * ROW:(i + 1) * HALVES * ROW] for i in range(7)] + [alias(xin[1], 0, HALVES * ROW)]
        zr = [a.rearrange("p (s f) -> p s f", s=HALVES) for a in zplace]
        ye = [alias(xin[0], i * HALVES * D, (i + 1) * HALVES * D).rearrange("p (s f) -> p s f", s=HALVES) for i in range(4)]
        zflat = [a[:, :, :, :].rearrange("p a b c -> p (a b c)") for a in zrow]
        wst = [a.rearrange("p (k n) -> p k n", k=2) for a in
               [zT[:, :], hpc[:, :, :].rearrange("p a b -> p (a b)"), alias(h[1], 0, 1024), alias(xc[1], 0, 1024)]
               + [f[:, k:k + 1024] for f in zflat for k in (0, 1024)]]
        padflat = alias(adjs[0], 0, PADS * HALVES * ROW)
        padrow = padflat.rearrange("p (k s f) -> p k s f", k=PADS, s=HALVES)
        xlast = [adjs[0][:, b, :].rearrange("p (t d) -> p t d", t=T) for b in range(NB)]
        ylast = [a.rearrange("p (t k d) -> p t k d", t=T, k=TOPK) for a in
                 [alias(adjs[1], k * 2 * NODES, (k + 1) * 2 * NODES) for k in range(4)] + [f[:, 0:2 * NODES] for f in zflat]]
        h32 = [alias(n1[i], 0, 1024) for i in range(2)]
        h16 = [alias(a, 0, 1024).bitcast(f16).rearrange("p (k n) -> p k n", k=2) for a in (dif, z, x3[0], x3[1])]
        zTe = [hT[:, 256 * i:256 * i + 256].bitcast(f16) for i in range(2)]
        yT = [hT[:, 512 + 256 * i:768 + 256 * i] for i in range(2)]
        le = alias(n1[0], 0, NTILES * E).rearrange("p (i e) -> p i e", e=E)
        le2 = alias(n1[1], 0, NTILES * E).rearrange("p (i e) -> p i e", e=E)
        gt = alias(dif, 0, E * (NTOK // TILE)).rearrange("p (e k) -> p e k", e=E)
        tt = hT[:, 0:4 * E].rearrange("p (k e) -> p k e", e=E)
        ti = hT[:, 512:512 + 4 * NTILES].rearrange("p (k i) -> p k i", i=NTILES)

        bank = [ctx.enter_context(nc.psum_tensor(f"bank{i}", [P, 512], f32)) for i in range(8)]
        acc, trb, hb, pb = bank[0:2], bank[2:4], bank[4:6], bank[6:8]
        zt_ps = [a[:, 0:256].bitcast(f16) for a in trb]
        hid_ps = [[bank[0], bank[1]], [bank[4], bank[5]]]
        yT_ps, y_ps = pb[0], pb[1]

        s_par, s_prep, s_prepT, s_tab, s_tabc = (
            sem(n) for n in ("s_par", "s_prep", "s_prepT", "s_tab", "s_tabc"))

        class Layer:
            def __init__(self, l):
                self.l = l
                s = lambda n: sem(f"l{l}_{n}")
                self.x_in = [s("x_in0"), s("x_in1")]
                self.adj_in = [[s(f"adj_in{i}{c}") for c in range(4)] for i in range(2)]
                self.bn, self.nrm, self.cmb = [s("bn1"), s("bn2")], s("nrm"), s("cmb")
                self.r1, self.r2, self.zl = s("r1"), s("r2"), s("zl")
                self.norm, self.kept = [s("norm1"), s("norm2")], s("kept")
                self.t1_ready, self.t1_done, self.t2_ready, self.t2_done = (
                    s("t1_ready"), s("t1_done"), s("t2_ready"), s("t2_done"))
                self.h_ready, self.h_done, self.acc_ready, self.acc_done = (
                    s("h_ready"), s("h_done"), s("acc_ready"), s("acc_done"))
                self.hT_ready, self.hp_ready, self.gate_e = s("hT_ready"), s("hp_ready"), s("gate_e")
                self.x3_stored, self.zhi = [s("x3_st0"), s("x3_st1")], s("zhi")
                self.lg_ready, self.rt_e, self.rank_ready = s("lg_ready"), s("rt_e"), s("rank_ready")
                self.scat, self.pads, self.reset = [s("scat0"), s("scat1")], s("pads"), s("reset")
                self.zrow_free = s("zrow_free")
                self.spare, self.pad_built = s("spare"), s("pad_built")
                self.w_in, self.w_hi, self.w_lo = s("w_in"), s("w_hi"), s("w_lo")
                self.b1_ps, self.b1_done = s("b1_ps"), s("b1_done")
                self.zt_ready, self.zt_done, self.hps, self.gelu = s("zt_ready"), s("zt_done"), s("hps"), s("gelu")
                self.hhi, self.h16 = s("hhi"), s("h16")
                self.yT_ps, self.yT_done, self.y_ps, self.y_done = s("yT_ps"), s("yT_done"), s("y_ps"), s("y_done")

        LY = [Layer(0), Layer(1)]
        zr_in, y_st = [sem(f"zr_in{i}") for i in range(8)], [sem(f"y_st{i}") for i in range(8)]
        ROUNDS = NTILES // 8
        f_x, f_y, f_sum, f_out = sem("f_x"), [sem(f"f_y{i}") for i in range(len(ylast))], sem("f_sum"), sem("f_out")
        f_add, s_tick = sem("f_add"), sem("s_tick")

        class Steps:
            def __init__(self, eng, s, per_call):
                self.eng, self.s, self.per = eng, s, per_call

            def begin(self, call):
                self.first, self.k = call * self.per, 0

            def put(self, ins, by=1):
                ins.then_inc(self.s, by)
                self.k += by

            def sync(self):
                self.eng.wait_ge(self.s, self.first + self.k)

            def link(self, ins):
                self.put(ins)
                yield
                self.sync()

            def end(self):
                assert self.k == self.per, (self.k, self.per)

        def write(*stages):
            stages = list(stages)
            while stages:
                stages = [s for s in stages if next(s, stages) is not stages]

        def batches(eng, step):
            step(0, 0, 0, 0)
            step(1, 0, 1, 1)
            with eng.Fori(1, NB // 2 - 1) as u:
                step(2 * u, u, 0, 2)
                step(2 * u + 1, u, 1, 3)
            step(NB - 2, NB // 2 - 1, 0, NB - 2)
            step(NB - 1, NB // 2 - 1, 1, NB - 1)

        def tiles(eng, step, engine=None):
            def run(first, u, least):
                before = 2 if least else 0
                if engine is not None:
                    _, e = nc.values_load_multi_w_load_instructions(
                        tab[0:1, 0, ds(first - before, 8 + before)], engines=[engine], min_val=0, max_val=E - 1,
                        skip_runtime_bounds_check_because="tables() takes their minimum with E - 1")
                for j in range(8):
                    step(first + j, u, j, least + j,
                         [e[j + before - k] if j + before >= k else None for k in range(3)] if engine is not None else None)
                return [e[-1], e[-2]] if engine is not None else None
            run(0, 0, 0)
            with eng.Fori(1, NTILES // 8 - 1) as u:
                run(8 * u, u, 8)
            return run(NTILES - 8, NTILES // 8 - 1, NTILES - 8)

        block = ctx.enter_context(nc.Block())

        @block.sync
        def _(sp):
            sp.dma_start(par[:, :], params).then_inc(s_par, 16)

            def load_x(l, b, u, j, least):
                y = LY[l]
                if least >= 2:
                    sp.wait_ge(y.kept, b - 1)
                src = x_v if l == 0 else xs_v[0]
                sp.dma_start(xin[j][:, :, :], src[ds(b * P, P), :, :]).then_inc(y.x_in[j], 16)
                if l == 1:
                    if least >= 1:
                        sp.wait_ge(y.bn[0], BN1_ALL[1] * (b - 1) + Y_ADDED)
                    sp.dma_start(yin[:, :, :, :], yq_v[0][ds(b * P, P), :, :, :]).then_inc(y.x_in[j], 16)

            def load_adj(l, b, u, j, least, chunks=range(4)):
                y = LY[l]
                if least >= 2:
                    sp.wait_ge(y.acc_ready, 2 * b - 2)
                elif l == 1:
                    sp.wait_ge(LY[0].acc_ready, 2 * NB)
                for c in chunks:
                    sp.dma_start(adjs[j][:, 2 * c:2 * c + 2, :],
                                 adj[ds(b * T + 2 * c, 2), :, :].rearrange("t p i -> p t i")).then_inc(y.adj_in[j][c], 16)

            def load_weights(l, experts=range(E)):
                for e in experts:
                    sp.dma_start(wst[e][:, 0, 0:HID[l]], w1_d[l][e]).then_inc(LY[l].w_in, 16)
                    sp.dma_start(wst[e][:, 1, 0:HID[l]], w2_d[l][e]).then_inc(LY[l].w_in, 16)

            def store_x3(l, b, j):
                sp.wait_ge(LY[l].cmb, CMB_ALL[l] * (b + 1))
                sp.dma_start(xs_v[l][ds(b * P, P), :, :], x3[j][:, :, :]).then_inc(LY[l].x3_stored[j], 16)

            def graph(l):
                if l == 1:
                    for s in y_st:
                        sp.wait_ge(s, 32 * ROUNDS)
                    for s in LY[0].x3_stored:
                        sp.wait_ge(s, FREE + 16 * (NB // 2))
                load_x(l, 0, 0, 0, 0)
                load_x(l, 1, 0, 1, 1)
                if l == 0:
                    load_weights(0)
                    load_adj(l, 0, 0, 0, 0)
                load_adj(l, 1, 0, 1, 1)

                def step(b, u, j, least):
                    if least < NB - 2:
                        load_x(l, b + 2, u + 1, j, least + 2)
                    if 1 <= least < NB - 1:
                        load_adj(l, b + 1, u + j, 1 - j, least + 1)
                    if least >= 1:
                        store_x3(l, b - 1, 1 - j)
                batches(sp, step)
                store_x3(l, NB - 1, 1)

            def experts(l):
                y = LY[l]
                if l == 0:
                    sp.wait_ge(y.lg_ready, NB)
                    sp.wait_ge(y.cmb, CMB_ALL[0] * NB)
                    load_weights(1, range(E // 2))
                sp.wait_ge(s_tab, 3 * (l + 1))
                sp.wait_ge(y.pad_built, 2)
                for e in range(E):
                    first = sp.value_load(padtab[0:1, e:e + 1], min_val=e * REGION, max_val=e * REGION + NTOK)
                    sp.dma_start(zq[l][ds(first, TILE), :].rearrange("(s p) f -> p s f", p=P),
                                 padrow[:, e, :, :]).then_inc(y.pads, 16)
                for k in range(NSPARE):
                    sp.dma_start(zq[l][SPARE + k * TILE:SPARE + (k + 1) * TILE, :].rearrange("(s p) f -> p s f", p=P),
                                 padrow[:, E + k, :, :]).then_inc(y.spare, 16)
                sp.wait_ge(y.pads, 16 * E)
                for s in y.scat:
                    sp.wait_ge(s, 16 * TOPK * T * (NB // 2))

                for s in y.x3_stored:
                    sp.wait_ge(s, FREE + 16 * (NB // 2))

                def step(i, u, j, least, e):
                    row = sp.value_load(tab[0:1, 1, ds(i, 1)], min_val=0, max_val=ZROWS - TILE)
                    if least >= 8:
                        sp.wait_ge(y_st[j], 32 * (ROUNDS * l + u))
                    if least == NTILES - NSPARE:
                        sp.wait_ge(y.spare, 16 * NSPARE)
                    sp.dma_start(zr[j][:, :, :], zq[l][ds(row, TILE), :].rearrange("(s p) f -> p s f", p=P))\
                        .then_inc(zr_in[j], 16)
                    if l == 0 and least == 7:
                        load_weights(1, range(E // 2, E))
                    c = least - (NTILES - 8)
                    if l == 0 and c >= 0 and c % 2 == 0:
                        load_adj(1, 0, 0, 0, 0, (c // 2,))
                    b = least - (NTILES - NB)
                    if l == 1 and b >= 0:
                        sp.dma_start(xlast[b], xs_v[1][b * P:(b + 1) * P, :, :]).then_inc(f_x, 16)
                assert NSPARE <= 8
                tiles(sp, step)

            graph(0)
            experts(0)
            graph(1)
            experts(1)

            for s in y_st:
                sp.wait_ge(s, 32 * 2 * ROUNDS)

            for b in range(NB):
                k = b % len(ylast)
                if b >= len(ylast):
                    sp.wait_ge(f_sum, b - len(ylast) + 1)
                sp.dma_start(ylast[k], yq_v[1][b * P:(b + 1) * P, :, :, :]).then_inc(f_y[k], 16)

        @block.scalar
        def _(act):
            def fetch_table(func, k):
                act.activation(warm[:, k:k + 1], col("ones")[:, 0:1], func)

            def normalise(y, i, n, dst, src):
                act.wait_ge(y.nrm, NRM_ALL[y.l] * (n + 3 * i) + NRM_RATE[y.l])
                for t in range(T):
                    ins = act.activation(dst[:, t, :], src[:, t, :], ACT.Identity,
                                         bias=ln_m[:, i, t:t + 1], scale=ln_r[:, i, t:t + 1])
                ins.then_inc(y.norm[i], 1)

            def ln1(l, n, j, least):
                y = LY[l]
                if least >= 2:
                    act.wait_ge(y.cmb, CMB_ALL[l] * (n - 2) + CMB_USED[l])
                normalise(y, 0, n, n1[j], xin[j])

            def weights_done(l):
                act.wait_ge(LY[l].w_lo, 2 * E)
                act.wait_ge(LY[l].b1_ps, E)

            def keep(l, j):
                act.activation(xc[j][:, :, :], xin[j][:, :, :], ACT.Copy).then_inc(LY[l].kept, 1)

            def t1_evac(l, n):
                y = LY[l]
                for hf in range(2):
                    act.wait_ge(y.t1_ready, 2 * n + hf + 1)
                    act.activation(n1T[:, 512 * hf:512 * hf + 512], trb[hf][:, :], ACT.Copy).then_inc(y.t1_done, 1)

            def t2_evac(l, n):
                y = LY[l]
                for hf in range(2):
                    act.wait_ge(y.t2_ready, 2 * n + hf + 1)
                    act.activation(zT[:, 512 * hf:512 * hf + 512], trb[hf][:, :], ACT.Copy).then_inc(y.t2_done, 1)

            def ln2(l, n, j, least):
                y = LY[l]
                if least >= 1:
                    act.wait_ge(y.zl, ZL_ALL * n)
                normalise(y, 1, n, z, x3[j])

            def high_parts(l, n, j):
                y = LY[l]
                act.wait_ge(y.norm[1], n + 1)
                act.wait_ge(y.zrow_free, FREE + n - 1)
                act.activation(zrow16[j][:, :, 0, 0:D], z[:, :, :], ACT.Copy).then_inc(y.zhi, 1)

            def gate_exp(n):
                act.wait_ge(LY[0].cmb, CMB_ALL[0] * n + CMB_USED[0])
                act.activation(ge[:, :], gl[:, :], ACT.Exp, scale=-1.0).then_inc(LY[0].gate_e, 1)

            def acc_evac(l, b, least, hf):
                y = LY[l]
                act.wait_ge(y.acc_ready, 2 * b + hf + 1)
                if not (least == 0 and hf == 0):
                    act.wait_ge(y.hT_ready, 2 * b + hf)
                if l == 0:
                    act.activation(hpc[:, 0, :], acc[hf][:, :], ACT.Copy).then_inc(y.acc_done, 1)
                else:
                    act.activation(hpc[:, 0, :], acc[hf][:, :], ACT.Relu)
                    act.activation(hpc[:, 1, :], acc[hf][:, :], ACT.Relu, scale=-1.0).then_inc(y.acc_done, 1)

            def routing_exp(l, n):
                y = LY[l]
                act.wait_ge(y.r1, R1_ALL[l] * n + R1_GAP[l])
                act.activation(rt_e[:, :], rt_d[:, :], ACT.Exp).then_inc(y.rt_e, 1)

            def weights_hi(l):
                y = LY[l]
                act.wait_ge(y.w_in, 32 * E)
                for e in range(E):
                    act.activation(w1q[l][:, e, 0, :], wst[e][:, 0, 0:HID[l]], ACT.Copy,
                                   scale=g64[:, l, e:e + 1]).then_inc(y.w_hi, 1)
                    act.activation(w2q[l][:, e, 0, :], wst[e][:, 1, 0:HID[l]], ACT.Copy,
                                   scale=WSCALE).then_inc(y.w_hi, 1)

            def graph(l):
                y = LY[l]
                if l == 1:
                    weights_hi(l)
                ln1(l, 0, 0, 0)
                keep(l, 0)
                t1_evac(l, 0)
                if l == 0:
                    weights_hi(l)
                ln1(l, 1, 1, 1)
                weights_done(l)
                keep(l, 1)
                def step(b, u, j, least):
                    if least >= 2:
                        high_parts(l, b - 2, j)
                        t2_evac(l, b - 2)
                    if least >= 1:
                        if l == 0:
                            gate_exp(b - 1)
                        if least < NB - 1:
                            ln1(l, b + 1, 1 - j, least + 1)
                    if least >= 2:
                        routing_exp(l, b - 2)
                    if 1 <= least < NB - 1:
                        keep(l, 1 - j)
                    acc_evac(l, b, least, 0)
                    if least < NB - 1:
                        t1_evac(l, b + 1)
                    acc_evac(l, b, least, 1)
                    if least >= 1:
                        ln2(l, b - 1, 1 - j, least - 1)
                batches(act, step)
                high_parts(l, NB - 2, 0)
                t2_evac(l, NB - 2)
                if l == 0:
                    gate_exp(NB - 1)
                routing_exp(l, NB - 2)
                ln2(l, NB - 1, 1, NB - 1)
                t2_evac(l, NB - 1)
                high_parts(l, NB - 1, 1)
                routing_exp(l, NB - 1)

            def experts(l):
                y = LY[l]
                fetch_table(ACT.Gelu, l + 1)
                act.wait_ge(s_tab, 3 * (l + 1))

                def gelu(i, e, least):
                    k = least % 2
                    if least >= 2:
                        act.wait_ge(y.h16, i - 1)
                    for c in range(CH[l]):
                        if c % 2 == 0:
                            act.wait_ge(y.hps, CH[l] // 2 * i + c // 2 + 1)
                        ins = act.activation(h32[k][:, 256 * c:256 * c + 256],
                                             hid_ps[k][c // 2][:, 256 * (c % 2):256 * (c % 2) + 256], ACT.Gelu,
                                             bias=b1tab[l][:, ds(e * CH[l] + c, 1)], scale=1.0 / WSCALE)
                        if c % 2 == 1:
                            ins.then_inc(y.gelu, 1)

                def yt(i, e, least):
                    act.wait_ge(y.yT_ps, i + 1)
                    act.activation(yT[least % 2], yT_ps[:, 0:TILE], ACT.Identity,
                                   bias=col(f"b2_{l}")[:, ds(e, 1)], scale=1.0 / WSCALE).then_inc(y.yT_done, 1)

                def step(i, u, j, least, e):
                    gelu(i, e[0], least)
                    if least >= 2:
                        yt(i - 2, e[2], least - 2)
                e = tiles(act, step, mybir.EngineType.Activation)
                yt(NTILES - 2, e[1], NTILES - 2)
                yt(NTILES - 1, e[0], NTILES - 1)

            act.wait_ge(s_par, 16)
            fetch_table(ACT.Exp, 0)
            act.wait_ge(s_prep, NPREP)
            for l in range(2):
                graph(l)
                experts(l)
            for b in range(NB):
                act.wait_ge(f_sum, b + 1)
                act.dma_start(out_v[b * P:(b + 1) * P, :, :], xlast[b]).then_inc(f_out, 16)
            act.wait_ge(f_out, 16 * NB)

        @block.tensor
        def _(pe):
            ident = col("ident_gate")[:, 0:P]

            def t1(l, n, least):
                y, j = LY[l], least % 2
                pe.wait_ge(y.norm[0], n + 1)
                for hf in range(2):
                    for t in range(4):
                        ins = pe.transpose(trb[hf][:, t * P:t * P + P], n1[j][:, 4 * hf + t, :], ident)
                    ins.then_inc(y.t1_ready, 1)

            def h_rows(l, n, least, groups):
                y = LY[l]
                w = col(f"wt{l}")
                for g in groups:
                    a, b = GROUPS[g]
                    pe.wait_ge(y.t1_done, 2 * n + (1 if g == 0 else 2))
                    if least >= 3 and g == 0:
                        pe.wait_ge(y.r2, R2_ALL * (n - 3) + R2_BASE)
                    if g == 2:
                        pe.wait_ge(y.h_done, 3 * n + 1)
                    for t in range(a, b):
                        ins = pe.matmul(hb[g % 2][:, (t - a) * (D + 1):(t - a) * (D + 1) + w.shape[1]],
                                        n1T[:, t * P:t * P + P], w, start=True, stop=True)
                    ins.then_inc(y.h_ready, 1)

            def aggregate(l, b, u, least, first, last):
                y, j = LY[l], least % 2
                for k in range(first, last):
                    hf, t = divmod(k, T)
                    if k == 0:
                        pe.wait_ge(y.h_done, 3 * b + 3)
                    if t == 0 and not (least == 0 and hf == 0):
                        pe.wait_ge(y.acc_done, 2 * b - 1 + hf)
                    if t % 2 == 0 and hf == 0:
                        pe.wait_ge(y.adj_in[j][t // 2], 16 * u + 16)
                    ins = pe.matmul(acc[hf][:, :], h[j][:, t, 0:D], adjs[j][:, t, 512 * hf:512 * hf + 512],
                                    start=(t == 0), stop=(t == T - 1))
                    if t == T - 1:
                        ins.then_inc(y.acc_ready, 1)

            def hp_rows(l, n, least, groups):
                y = LY[l]
                for g in groups:
                    a, c = GROUPS[g]
                    if least >= 1 and g == 0:
                        pe.wait_ge(y.cmb, CMB_ALL[l] * (n - 1) + CMB_USED[l])
                    if g == 2:
                        pe.wait_ge(y.cmb, CMB_ALL[l] * n + CMB_GROUP[l])
                    else:
                        pe.wait_ge(y.hT_ready, 2 * n + g + 1)
                    for t in range(a, c):
                        o = (t - a) * (D + 1) if l == 0 else (t - a) * D
                        if l == 0:
                            ins = pe.matmul(pb[g % 2][:, o:o + D + 1], hT[:, t * P:t * P + P],
                                            col("ident_gate"), start=True, stop=True)
                        else:
                            ins = pe.transpose(pb[g % 2][:, o:o + D], hT[:, t * P:t * P + P], ident)
                    ins.then_inc(y.hp_ready, 1)

            def t2(l, n):
                y = LY[l]
                pe.wait_ge(y.norm[1], n + 1)
                for hf in range(2):
                    for t in range(4):
                        ins = pe.transpose(trb[hf][:, t * P:t * P + P], z[:, 4 * hf + t, :], ident)
                    ins.then_inc(y.t2_ready, 1)

            def logits(l, n, last):
                y = LY[l]
                w = gwr[:, :] if l == 0 else col("wr1")
                pe.wait_ge(y.t2_done, 2 * n + 2)
                if last:
                    pe.wait_ge(y.r1, R1_ALL[l] * (n - 1) + R1_LOGITS)
                for t in range(T):
                    ins = pe.matmul(hb[1][:, t * E:t * E + E], zT[:, t * P:t * P + P], w, start=True, stop=True)
                ins.then_inc(y.lg_ready, 1)

            def ranks(l, n, last):
                y = LY[l]
                pe.wait_ge(y.r1, R1_ALL[l] * (n + 1))
                if last:
                    pe.wait_ge(y.r2, R2_ALL * (n - 1) + R2_BASE)
                pe.matmul(hb[0][:, 0:(T + 1) * E], tri16[:, :], M[:, :, :], start=True, stop=False)
                for t in range(T):
                    ins = pe.matmul(hb[0][:, (t + 1) * E:(T + 1) * E], ones16[:, :],
                                    M[:, t:t + 1, :].to_broadcast([P, T - t, E]), start=False, stop=(t == T - 1))
                ins.then_inc(y.rank_ready, 1)

            def graph(l):
                y = LY[l]
                def expert_biases():
                    pe.wait_ge(y.w_in, 32 * E)
                    for e in range(E):
                        beta = col("beta") if l == 0 else col("lnb")[:, e:e + 1]
                        for c in range(CH[l]):
                            k = e * CH[l] + c
                            ins = pe.matmul(pb[1][:, k:k + 1], wst[e][:, 0, c * P:c * P + P], beta,
                                            start=True, stop=True)
                        ins.then_inc(y.b1_ps, 1)

                if l == 1:
                    pe.wait_ge(LY[0].y_done, NTILES)
                    expert_biases()
                t1(l, 0, 0)
                h_rows(l, 0, 0, (0, 1, 2))

                def step(b, u, j, least):
                    go = lambda first, last: aggregate(l, b, u, least, first, last)
                    go(0, 2)
                    if least == 0 and l == 0:
                        expert_biases()
                    if least == 1:
                        pe.wait_ge(y.b1_done, 1)
                        pe.wait_ge(s_prep, NPREP + 1)
                    if least >= 1:
                        hp_rows(l, b - 1, least - 1, (0, 1))
                    go(2, 3)
                    if least >= 2:
                        t2(l, b - 2)
                    if least >= 1:
                        hp_rows(l, b - 1, least - 1, (2,))
                    go(3, 5)
                    if least >= 2:
                        logits(l, b - 2, False)
                    go(5, 11)
                    if least < NB - 1:
                        t1(l, b + 1, least + 1)
                    if least >= 2:
                        ranks(l, b - 2, False)
                    go(11, 13)
                    if least < NB - 1:
                        h_rows(l, b + 1, least + 1, (0, 1))
                    go(13, 15)
                    if least < NB - 1:
                        h_rows(l, b + 1, least + 1, (2,))
                    go(15, 16)
                batches(pe, step)
                hp_rows(l, NB - 1, NB - 1, (0, 1))
                t2(l, NB - 2)
                hp_rows(l, NB - 1, NB - 1, (2,))
                logits(l, NB - 2, True)
                ranks(l, NB - 2, True)
                t2(l, NB - 1)
                logits(l, NB - 1, True)
                ranks(l, NB - 1, True)

            def experts(l):
                y = LY[l]
                nb = CH[l] // 2
                pe.wait_ge(s_tab, 3 * (l + 1))

                def turn(i, u, least):
                    j, k = least % 8, least % 2
                    pe.wait_ge(zr_in[j], 16 * (ROUNDS * l + u + 1))
                    rows = zr[j][:, :, :].bitcast(f16)
                    for v in range(2):
                        for s in range(HALVES):
                            ins = pe.transpose(zt_ps[k][:, (2 * v + s) * P:(2 * v + s + 1) * P],
                                               rows[:, s, v * D:v * D + D], ident16[:, :])
                    ins.then_inc(y.zt_ready, 1)

                def up(i, e, least):
                    k = least % 2
                    pe.wait_ge(y.zt_done, i + 1)
                    if least >= 2:
                        pe.wait_ge(y.gelu, nb * (i - 1))
                    for c in range(CH[l]):
                        o = hid_ps[k][c // 2][:, 256 * (c % 2):256 * (c % 2) + 256]
                        for n, (w, v) in enumerate(((0, 0), (0, 1), (1, 0))):
                            ins = pe.matmul(o, w1q[l][:, ds(e, 1), w, c * P:c * P + P],
                                            zTe[k][:, 256 * v:256 * v + 256], start=(n == 0), stop=(n == 2))
                        if c % 2 == 1:
                            ins.then_inc(y.hps, 1)

                def down(i, e, least):
                    k = least % 4
                    pe.wait_ge(y.h16, i + 1)
                    for c in range(CH[l]):
                        for n, (w, v) in enumerate(((0, 0), (0, 1), (1, 0))):
                            ins = pe.matmul(yT_ps[:, 0:TILE], w2q[l][:, ds(e, 1), w, c * P:c * P + P],
                                            h16[k][:, v, 256 * c:256 * c + 256],
                                            start=(c == 0 and n == 0), stop=(c == CH[l] - 1 and n == 2))
                    ins.then_inc(y.yT_ps, 1)

                def turn_back(i, least):
                    k = least % 2
                    pe.wait_ge(y.yT_done, i + 1)
                    if least >= 1:
                        pe.wait_ge(y.y_done, i)
                    for s in range(HALVES):
                        ins = pe.transpose(y_ps[:, s * P:s * P + P], yT[k][:, s * P:s * P + P], ident)
                    ins.then_inc(y.y_ps, 1)

                turn(0, 0, 0)

                def step(i, u, j, least, e):
                    if least < NTILES - 1:
                        turn(i + 1, u + (j == 7), least + 1)
                    up(i, e[0], least)
                    if least >= 3:
                        turn_back(i - 3, least - 3)
                    if least >= 2:
                        down(i - 2, e[2], least - 2)
                e = tiles(pe, step, mybir.EngineType.PE)
                turn_back(NTILES - 3, NTILES - 3)
                down(NTILES - 2, e[1], NTILES - 2)
                turn_back(NTILES - 2, NTILES - 2)
                down(NTILES - 1, e[0], NTILES - 1)
                turn_back(NTILES - 1, NTILES - 1)

            pe.wait_ge(s_par, 16)
            pe.wait_ge(s_prep, NPREP)
            pe.matmul(pb[0][:, 0:E], beta_b[:, :], col("wr0"), start=True, stop=True).then_inc(s_prepT, 1)
            for l in range(2):
                graph(l)
                experts(l)

        @block.vector
        def _(dve):
            V = nc.vector
            bc = lambda a, n: a.unsqueeze(2).to_broadcast([P, a.shape[1], n])
            bt = lambda a, n: a.unsqueeze(1).to_broadcast([P, n, a.shape[1]])
            tt_ = V.tensor_tensor

            def norms(y, m, least, first, second, steps):
                a, c = (0 if first else 1), (2 if second else 1)
                top = c + (second and y.l == 1)
                steps.begin(m)
                (mu, q), (mu_, q_) = ((st[:, a:c, :, k + 1], st[:, a:c, :, k + 2]) for k in (0, 3))
                two_mean, gap, var = (mv[:, k, a:c, :] for k in range(3))
                steps.put(tt_(two_mean, mu, mu_, ALU.add))
                steps.put(tt_(gap, mu, mu_, ALU.subtract))
                yield from steps.link(tt_(var, q, q_, ALU.add))
                yield from steps.link(tt_(gap, gap, gap, ALU.mult))
                yield from steps.link(V.scalar_tensor_tensor(out=var, in0=gap, scalar=D / 4.0, in1=var,
                                                             op0=ALU.mult, op1=ALU.add))
                if first:
                    steps.put(V.tensor_scalar(ln_v[:, 0, :], mv[:, 2, 0, :], 1.0 / D, EPS, ALU.mult, ALU.add),
                              1 if second else 2 + y.l)
                if second:
                    steps.put(V.tensor_scalar(ln_v[:, 1, :], mv[:, 2, 1, :], (1.0 + EPS) / D, EPS * EPS,
                                              ALU.mult, ALU.add), 1 if first else 2)
                    if y.l == 1:
                        steps.put(V.tensor_scalar(ln_v[:, 2, :], mv[:, 2, 1, :], 1.0 / D, EPS, ALU.mult, ALU.add))
                yield
                steps.sync()
                if least >= 1:
                    dve.wait_ge(y.norm[0], NB if least > NB else m)
                if least >= 4:
                    dve.wait_ge(y.norm[1], m - 3)
                v, t, r = (x[:, a:top, :] for x in (ln_v, ln_t, ln_r))
                yield from steps.link(V.tensor_scalar(r.bitcast(i32), v.bitcast(i32), 1, None, ALU.logical_shift_right))
                yield from steps.link(V.tensor_scalar(r.bitcast(i32), r.bitcast(i32), -1.0, ROOT_GUESS, ALU.mult, ALU.add))
                for _ in range(NEWTON):
                    yield from steps.link(tt_(t, r, r, ALU.mult))
                    yield from steps.link(V.scalar_tensor_tensor(out=t, in0=t, scalar=-0.5, in1=v, op0=ALU.mult, op1=ALU.mult))
                    yield from steps.link(V.scalar_tensor_tensor(out=r, in0=t, scalar=1.5, in1=r, op0=ALU.add, op1=ALU.mult))
                steps.put(V.scalar_tensor_tensor(out=ln_m[:, a:c, :], in0=two_mean, scalar=-0.5,
                                                 in1=ln_r[:, a:c, :], op0=ALU.mult, op1=ALU.mult),
                          1 if second or y.l == 0 else 3)
                if second and y.l == 1:
                    assert steps.k == NRM_RATE[1]
                    yield from steps.link(tt_(zs[:, :], ln_v[:, 1, :], ln_r[:, 1, :], ALU.mult))
                    steps.put(tt_(zs[:, :], zs[:, :], ln_r[:, 2, :], ALU.mult))
                steps.end()

            def prepare():
                ops = [
                    V.tensor_copy(tri16[:, :], col("before")),
                    V.tensor_copy(ones16[:, :], col("ones")),
                    V.tensor_copy(ident16[:, :], col("ident_gate")[:, 0:P]),
                    V.tensor_scalar(gwr[:, :], col("wr0"), col("gamma"), None, ALU.mult),
                    V.tensor_scalar(beta_b[:, :], col("ones"), col("beta"), None, ALU.mult),
                    V.tensor_scalar(g64[:, 0, :], col("ones")[:, 0:E], col("gamma"), WSCALE, ALU.mult, ALU.mult),
                    V.tensor_scalar(g64[:, 1, :], col("lng"), WSCALE, None, ALU.mult),
                    V.tensor_scalar(nalpha[:, :], col("alpha"), -1.0, None, ALU.mult),
                    V.memset(M[:, :, :], 0.0),
                ]
                for ins in ops:
                    ins.then_inc(s_prep, 1)
                dve.wait_ge(s_prep, len(ops))
                assert len(ops) == NPREP
                dve.wait_ge(s_prepT, 1)
                tt_(br0f[:, :], pb[0][:, 0:E], col("br0"), ALU.add).then_inc(s_prep, 1)
                dve.wait_ge(s_prep, NPREP + 1)

            def graph(l):
                y = LY[l]
                bn = [Steps(dve, y.bn[0], BN1_ALL[l]), Steps(dve, y.bn[1], T)]
                nrm = Steps(dve, y.nrm, NRM_ALL[l])
                r1, r2 = Steps(dve, y.r1, R1_ALL[l]), Steps(dve, y.r2, R2_ALL)
                cmb, zl = Steps(dve, y.cmb, CMB_ALL[l]), Steps(dve, y.zl, ZL_ALL)
                W = D + 1 if l == 0 else D
                bias = col(f"bias{l}")

                def weights_lo():
                    for e in range(E):
                        dve.wait_ge(y.w_hi, 2 * (e + 1))
                        V.scalar_tensor_tensor(out=w1q[l][:, e, 1, :], in0=wst[e][:, 0, 0:HID[l]],
                                               scalar=g64[:, l, e:e + 1], in1=w1q[l][:, e, 0, :],
                                               op0=ALU.mult, op1=ALU.subtract).then_inc(y.w_lo, 1)
                        V.scalar_tensor_tensor(out=w2q[l][:, e, 1, :], in0=wst[e][:, 1, 0:HID[l]],
                                               scalar=WSCALE, in1=w2q[l][:, e, 0, :],
                                               op0=ALU.mult, op1=ALU.subtract).then_inc(y.w_lo, 1)
                    dve.wait_ge(y.b1_ps, E)
                    tt_(b1tab[l][:, :], pb[1][:, 0:E * CH[l]], col(f"b1_{l}"), ALU.add).then_inc(y.b1_done, 1)

                def stats_1(n, u, j):
                    bn[0].begin(n)
                    dve.wait_ge(y.x_in[j], (16 + 16 * l) * (u + 1))
                    if l == 1:
                        for k in range(TOPK):
                            yield from bn[0].link(tt_(xin[j][:, :, :], xin[j][:, :, :], yin[:, :, k, :], ALU.add))
                    for t in range(T):
                        bn[0].put(V.bn_stats(st[:, 0, t, :], xin[j][:, t, :]))
                        yield
                    bn[0].end()

                def stats_2(n, j):
                    bn[1].begin(n)
                    for t in range(T):
                        bn[1].put(V.bn_stats(st[:, 1, t, :], x3[j][:, t, :]))
                        yield
                    bn[1].end()

                def h_evac(n, least):
                    j = least % 2
                    if least >= 2:
                        dve.wait_ge(y.acc_ready, 2 * n - 2)
                    for g, (a, b) in enumerate(GROUPS):
                        dve.wait_ge(y.h_ready, 3 * n + g + 1)
                        src = hb[g % 2][:, 0:(b - a) * (D + 1)].rearrange("p (t w) -> p t w", w=D + 1)[:, :, 0:W]
                        tt_(h[j][:, a:b, 0:W], src, bt(bias, b - a), ALU.add).then_inc(y.h_done, 1)
                        yield

                def hT_evac(b, hf):
                    dve.wait_ge(y.acc_done, 2 * b + hf + 1)
                    o = hT[:, 512 * hf:512 * hf + 512]
                    if l == 0:
                        ins = V.scalar_tensor_tensor(out=o, in0=hpc[:, 0, :], scalar=0.2, in1=hpc[:, 0, :],
                                                     op0=ALU.mult, op1=ALU.max)
                    else:
                        ins = V.scalar_tensor_tensor(out=o, in0=hpc[:, 1, :], scalar=nalpha[:, 0:1],
                                                     in1=hpc[:, 0, :], op0=ALU.mult, op1=ALU.add)
                    ins.then_inc(y.hT_ready, 1)

                def route_1(n):
                    r1.begin(n)
                    dve.wait_ge(y.lg_ready, n + 1)
                    ps = hb[1][:, 0:T * E].rearrange("p (t e) -> p t e", e=E)
                    if l == 0:
                        yield from r1.link(tt_(lg[:, :, :], ps, bt(br0f[:, :], T), ALU.add))
                    else:
                        dve.wait_ge(y.nrm, NRM_ALL[1] * (n + 4))
                        yield from r1.link(tt_(lg[:, :, :], ps, bc(zs[:, :], E), ALU.mult))
                        yield from r1.link(tt_(lg[:, :, :], lg[:, :, :], bt(col("br1"), T), ALU.add))

                    def choose(src, m, oh):
                        yield from r1.link(tt_(cand[:, :, :], src[:, :, :], bc(m[:, :], E), ALU.is_equal))
                        yield from r1.link(tt_(cand[:, :, :], cand[:, :, :], bt(col("rev"), T), ALU.mult))
                        yield from r1.link(V.tensor_reduce(c1[:, :], cand[:, :, :], AX.X, ALU.max))
                        yield from r1.link(tt_(oh[:, :, :], bt(col("rev"), T), bc(c1[:, :], E), ALU.is_equal))

                    yield from r1.link(V.tensor_reduce(m1[:, :], lg[:, :, :], AX.X, ALU.max))
                    yield from choose(lg, m1, oh1)
                    yield from r1.link(V.scalar_tensor_tensor(out=eq[:, :, :], in0=oh1[:, :, :], scalar=-BIG,
                                                   in1=lg[:, :, :], op0=ALU.mult, op1=ALU.add))
                    yield from r1.link(V.tensor_reduce(m2[:, :], eq[:, :, :], AX.X, ALU.max))
                    r1.put(tt_(rt_d[:, :], m2[:, :], m1[:, :], ALU.subtract))
                    assert r1.k == R1_GAP[l]
                    yield from choose(eq, m2, oh2)
                    r1.put(tt_(M[:, 0:T, :], oh1[:, :, :], oh2[:, :, :], ALU.add))
                    r1.end()

                def route_2(n, j):
                    r2.begin(n)
                    w_out = zrow[j][:, :, :, D + 1]
                    dve.wait_ge(y.rt_e, n + 1)
                    yield from r2.link(V.tensor_scalar(rt_w[:, :], rt_e[:, :], 1.0, None, ALU.add))
                    yield from r2.link(V.reciprocal(rt_w[:, :], rt_w[:, :]))
                    r2.put(V.tensor_copy(w_out[:, :, 0], rt_w[:, :]))
                    r2.put(tt_(w_out[:, :, 1], rt_w[:, :], rt_e[:, :], ALU.mult))
                    dve.wait_ge(y.rank_ready, n + 1)
                    yield from r2.link(tt_(pos[:, :, :], hb[0][:, 0:T * E].rearrange("p (t e) -> p t e", e=E),
                                bt(base[:, :], T), ALU.add))
                    r2.put(tt_(base[:, :], base[:, :], hb[0][:, T * E:(T + 1) * E], ALU.add))
                    assert r2.k == R2_BASE
                    r2.put(tt_(pp[:, 0, :, :], pos[:, :, :], oh1[:, :, :], ALU.mult))
                    yield from r2.link(tt_(pp[:, 1, :, :], pos[:, :, :], oh2[:, :, :], ALU.mult))
                    for k in range(TOPK):
                        with nc.allow_low_precision(reason="whole numbers, exact in float32"):
                            r2.put(V.tensor_reduce(idx[j][:, :, k], pp[:, k, :, :], AX.X, ALU.add))
                    r2.end()

                def combine(b, u, j, groups):
                    if groups[0] == 0:
                        cmb.begin(b)
                        dve.wait_ge(y.x3_stored[j], FREE + 16 * u)
                    for g in groups:
                        a, c = GROUPS[g]
                        dve.wait_ge(y.hp_ready, 3 * b + g + 1)
                        ps = pb[g % 2][:, 0:(c - a) * W].rearrange("p (t w) -> p t w", w=W)
                        if l == 0:
                            cmb.put(tt_(dif[:, a:c, :], n1[j][:, a:c, :], ps[:, :, 0:D], ALU.subtract))
                            cmb.put(tt_(x3[j][:, a:c, :], xc[j][:, a:c, :], ps[:, :, 0:D], ALU.add))
                            cmb.put(tt_(gl[:, a:c], h[j][:, a:c, D], ps[:, :, D], ALU.add))
                        else:
                            cmb.put(tt_(x3[j][:, a:c, :], xc[j][:, a:c, :], ps, ALU.add))

                def gate(b, j):
                    dve.wait_ge(y.gate_e, b + 1)
                    yield from cmb.link(V.tensor_scalar(gc[:, :], ge[:, :], 1.0, None, ALU.add))
                    yield from cmb.link(V.reciprocal(gc[:, :], gc[:, :]))
                    for t in range(T):
                        cmb.put(V.scalar_tensor_tensor(out=x3[j][:, t, :], in0=dif[:, t, :], scalar=gc[:, t:t + 1],
                                                       in1=x3[j][:, t, :], op0=ALU.mult, op1=ALU.add))
                        yield

                def rows(b, j):
                    zl.begin(b)
                    dve.wait_ge(y.zhi, b + 1)
                    yield from zl.link(tt_(zrow16[j][:, :, 0, D:2 * D], z[:, :, :], zrow16[j][:, :, 0, 0:D], ALU.subtract))
                    zl.put(V.tensor_copy(zrow16[j][:, :, 1, 0:2 * D], zrow16[j][:, :, 0, 0:2 * D]))
                    yield from zl.link(V.tensor_copy(zrowu[j][:, :, :, D], tid[:, :].rearrange("p (t k) -> p t k", k=TOPK)))
                    zl.put(V.tensor_scalar(tid[:, :], tid[:, :], float(NODES * TOPK), None, ALU.add))
                    zl.end()

                V.tensor_copy(base[:, :], col("region")).then_inc(y.reset, 1)
                V.tensor_copy(tid[:, :], col("dest")).then_inc(y.reset, 1)
                for k, ring in enumerate(y.x3_stored + [y.zrow_free]):
                    V.memset(spark[:, k:k + 1], 0.0).then_inc(ring, FREE)
                dve.wait_ge(y.reset, 2)
                if l == 1:
                    weights_lo()
                write(stats_1(0, 0, 0))
                bn[0].sync()
                write(norms(y, 0, 0, True, False, nrm))
                write(stats_1(1, 0, 1))
                bn[0].sync()
                write(norms(y, 1, 1, True, False, nrm))
                write(h_evac(0, 0))
                if l == 0:
                    weights_lo()
                def step(b, u, j, least):
                    if least >= 1:
                        hT_evac(b - 1, 1)
                        combine(b - 1, u - (1 - j), 1 - j, (0, 1))
                    if least < NB - 2:
                        write(stats_1(b + 2, u + 1, j))
                    if least >= 1:
                        combine(b - 1, u - (1 - j), 1 - j, (2,))
                    if least >= 1:
                        if l == 0:
                            write(gate(b - 1, 1 - j))
                        cmb.sync()
                        cmb.end()
                    first, second, third = least < NB - 2, least >= 1, least >= 2
                    write(*([route_1(b - 2)] if third else []), *([stats_2(b - 1, 1 - j)] if second else []))
                    hT_evac(b, 0)
                    if first:
                        bn[0].sync()
                    if second:
                        bn[1].sync()
                    beside = [route_2(b - 2, j), rows(b - 2, j)] if third else []
                    if least < NB - 1:
                        beside.append(h_evac(b + 1, least + 1))
                    write(*([norms(y, b + 2, least + 2, first, second, nrm)] if first or second else []), chain(*beside))
                batches(dve, step)
                last = NB - 1
                hT_evac(last, 1)
                combine(last, NB // 2 - 1, 1, (0, 1, 2))
                if l == 0:
                    write(gate(last, 1))
                cmb.sync()
                cmb.end()

                def statistics_synced():
                    yield from stats_2(last, 1)
                    bn[1].sync()
                write(chain(statistics_synced(), norms(y, NB + 2, NB + 2, False, True, nrm)),
                      chain(rows(last - 1, 0), route_1(last - 1), route_2(last - 1, 0)))
                V.memset(padflat, 0.0).then_inc(y.pad_built, 1)
                dve.wait_ge(y.pad_built, 1)
                V.tensor_copy(padrow[:, :, :, D].bitcast(u32),
                              col("pad_dest").rearrange("p (k s) -> p k s", s=HALVES)).then_inc(y.pad_built, 1)
                write(rows(last, 1), route_1(last))
                write(route_2(last, 1))

            def tables(l):
                c = Steps(dve, s_tabc, 12)
                c.begin(l)
                dve.wait_ge(LY[l].r2, R2_ALL * NB)
                n, k, upto = tt[:, 0, :], tt[:, 1, :], tt[:, 2, :]
                c.put(V.memset(tt[:, 3, :], 0.0))
                yield from c.link(tt_(n, base[:, :], col("region"), ALU.subtract))
                yield from c.link(tt_(gt, bc(n, NTOK // TILE), bt(col("thresholds"), E), ALU.is_gt))
                yield from c.link(V.tensor_reduce(k, gt, AX.X, ALU.add))
                yield from c.link(V.tensor_tensor_scan(upto, k, tt[:, 3, :], 0.0, ALU.add, ALU.add))
                yield from c.link(tt_(le, bt(upto, NTILES), bc(col("tile_index"), E), ALU.is_le))
                yield from c.link(V.tensor_reduce(ti[:, 0, :], le, AX.X, ALU.add))
                yield from c.link(tt_(le2, le, bt(k, NTILES), ALU.mult))
                yield from c.link(V.tensor_reduce(ti[:, 1, :], le2, AX.X, ALU.add))
                yield from c.link(V.scalar_tensor_tensor(out=ti[:, 1, :], in0=ti[:, 1, :], scalar=-float(TILE),
                                              in1=col("tile_rows"), op0=ALU.mult, op1=ALU.add))
                yield from c.link(V.scalar_tensor_tensor(out=ti[:, 1, :], in0=ti[:, 0, :], scalar=float(REGION),
                                              in1=ti[:, 1, :], op0=ALU.mult, op1=ALU.add))
                yield from c.link(V.tensor_scalar(ti[:, 0, :], ti[:, 0, :], float(E - 1), None, ALU.min))
                c.end()
                V.tensor_copy(tab[:, 0, :], ti[:, 0, :]).then_inc(s_tab, 1)
                V.tensor_copy(tab[:, 1, :], ti[:, 1, :]).then_inc(s_tab, 1)
                V.tensor_copy(padtab[:, :], base[:, :]).then_inc(s_tab, 1)

            def experts(l):
                y = LY[l]
                nb = CH[l] // 2
                dve.wait_ge(s_tab, 3 * (l + 1))

                def z_evac(i, least):
                    k = least % 2
                    dve.wait_ge(y.zt_ready, i + 1)
                    if least >= 2:
                        dve.wait_ge(y.hps, nb * (i - 1))
                    V.tensor_copy(zTe[k], zt_ps[k]).then_inc(y.zt_done, 1)

                def split(i, least):
                    k, n = least % 2, HID[l] * TILE // P
                    o = h16[least % 4]
                    dve.wait_ge(y.gelu, nb * (i + 1))
                    V.tensor_copy(o[:, 0, 0:n], h32[k][:, 0:n]).then_inc(y.hhi, 1)
                    dve.wait_ge(y.hhi, i + 1)
                    tt_(o[:, 1, 0:n], h32[k][:, 0:n], o[:, 0, 0:n], ALU.subtract).then_inc(y.h16, 1)

                def y_evac(i, u, least):
                    j = least % 4
                    dve.wait_ge(y.y_ps, i + 1)
                    if least >= 4:
                        dve.wait_ge(y_st[(least - 4) % 8], 32 * (ROUNDS * l + u + 1))
                    for s in range(HALVES):
                        ins = V.tensor_scalar(ye[j][:, s, :], y_ps[:, s * P:s * P + P],
                                              zr[least % 8][:, s, D + 1:D + 2], None, ALU.mult)
                    ins.then_inc(y.y_done, 1)

                z_evac(0, 0)

                def step(i, u, j, least, e):
                    if least < NTILES - 1:
                        z_evac(i + 1, least + 1)
                    if least >= 1:
                        split(i - 1, least - 1)
                    if least >= 3:
                        y_evac(i - 3, u - (j < 7), least - 3)
                tiles(dve, step)
                y_evac(NTILES - 3, (NTILES - 7) // 8, NTILES - 3)
                split(NTILES - 1, NTILES - 1)
                y_evac(NTILES - 2, (NTILES - 6) // 8, NTILES - 2)
                y_evac(NTILES - 1, (NTILES - 5) // 8, NTILES - 1)

            dve.wait_ge(s_par, 16)
            prepare()
            for l in range(2):
                graph(l)
                write(tables(l))
                experts(l)
            dve.wait_ge(f_x, 16 * NB)
            for b in range(NB):
                y0y1 = ylast[b % len(ylast)]
                dve.wait_ge(f_y[b % len(ylast)], 16 * (b // len(ylast) + 1))
                tt_(xlast[b], xlast[b], y0y1[:, :, 0, :], ALU.add).then_inc(f_add, 1)
                dve.wait_ge(f_add, b + 1)
                tt_(xlast[b], xlast[b], y0y1[:, :, 1, :], ALU.add).then_inc(f_sum, 1)

        @block.gpsimd
        def _(pool):
            def signal_free(y, b, u, j):
                pool.wait_ge(y.scat[1 - j], 16 * TOPK * T * (u + j))
                pool.tensor_tensor(tick[:, 3:4], tick[:, 0:1], tick[:, 1:2], ALU.add).then_inc(y.zrow_free, 1)

            def pass_on(call):
                pool.wait_ge(s_tick, call + 1)
                pool.tensor_tensor(tick[:, 2:3], tick[:, 0:1], tick[:, 1:2], ALU.add).then_inc(s_tick, 1)

            pool.wait_ge(s_par, 16)
            pool.memset(tick[:, :], 0.0).then_inc(s_tick, 1)
            pool.wait_ge(s_tick, 1)
            for l in range(2):
                y = LY[l]

                def send(b, u, j, least):
                    pool.wait_ge(y.zl, ZL_ALL * (b + 1))
                    pool.wait_ge(y.r2, R2_ALL * (b + 1))
                    pass_on(l * (NB + NTILES) + b)
                    for t in range(T):
                        if t == 1 and least >= 1:
                            signal_free(y, b, u, j)
                        for k in range(TOPK):
                            pool.indirect_dma_start(
                                out=zq[l], out_offset=bass.IndirectOffsetOnAxis(ap=idx[j][:, t, k:k + 1], axis=0),
                                in_=zrow[j][:, t, k, :], in_offset=None).then_inc(y.scat[j], 16)
                batches(pool, send)

                def give_back(i, u, j, least, e):
                    pool.wait_ge(y.y_done, i + 1)
                    pass_on(l * (NB + NTILES) + NB + i)
                    for s in range(HALVES):
                        pool.indirect_dma_start(
                            out=yq[l],
                            out_offset=bass.IndirectOffsetOnAxis(ap=zr[j][:, s, D:D + 1].bitcast(u32), axis=0),
                            in_=ye[j % 4][:, s, :], in_offset=None).then_inc(y_st[j], 16)
                tiles(pool, give_back)


def _columns(**given):
    import numpy as _np
    a = _np.zeros((P, NPARAM), _np.float32)
    for name, v in given.items():
        lo, hi = COL[name]
        a[:, lo:hi] = v
    return a


def kernel(**inputs):
    import numpy as _np
    import concourse.bacc as _bacc
    from concourse import mybir as _mybir
    from concourse.bass_utils import run_bass_kernel_spmd as _run

    g = {k: _np.asarray(v) for k, v in inputs.items()}
    row = lambda v: _np.broadcast_to(v.reshape(1, -1), (P, v.size))
    eye = _np.eye(P, dtype=_np.float32)
    p = _np.arange(P)
    gate = g["L0_gnn_gate_w"][0]
    params = _columns(
        wt0=_np.concatenate([g["L0_gnn_W_w"].T, gate[0:D, None]], axis=1),
        ident_gate=_np.concatenate([eye, gate[D:2 * D, None]], axis=1),
        bias0=row(_np.concatenate([g["L0_gnn_W_b"], g["L0_gnn_gate_b"]])),
        wt1=g["L1_gnn_W"].T, bias1=row(g["L1_gnn_b"]),
        wr0=g["L0_ffn_Wr"], br0=row(g["L0_ffn_br"]),
        gamma=g["L0_ffn_gamma"][:, None], beta=g["L0_ffn_beta"][:, None],
        wr1=g["L1_ffn_Wr"], br1=row(g["L1_ffn_br"]),
        lng=g["L1_ffn_ln_g"].T, lnb=g["L1_ffn_ln_b"].T,
        b1_0=g["L0_ffn_b1"].reshape(E * CH[0], P).T, b2_0=g["L0_ffn_b2"].T,
        b1_1=g["L1_ffn_b1"].reshape(E * CH[1], P).T, b2_1=g["L1_ffn_b2"].T,
        alpha=g["L1_gnn_alpha"].reshape(1, 1),
        before=(p[:, None] < p[None, :]), ones=1.0, rev=E - _np.arange(E), region=_np.arange(E) * REGION,
        dest=(p[:, None] * T * TOPK + _np.arange(T * TOPK)[None, :]),
        thresholds=_np.arange(NTOK // TILE) * TILE,
        tile_rows=_np.arange(NTILES) * TILE, tile_index=_np.arange(NTILES),
        pad_dest=NTOK * TOPK + _np.arange(PADS * HALVES)[None, :] * P + p[:, None],
    )
    adj = g["adj"].reshape(NB, P, T, P, T).transpose(0, 4, 3, 2, 1).reshape(NB * T, P, NODES)
    down = lambda w, l: w.reshape(E, CH[l], P, D).transpose(0, 2, 1, 3).reshape(E, P, HID[l])
    arrays = {
        "x": g["x"].reshape(NTOK, D), "adj": adj, "params": params,
        "w1_0": g["L0_ffn_W1"], "w2_0": down(g["L0_ffn_W2"], 0),
        "w1_1": g["L1_ffn_W1"], "w2_1": down(g["L1_ffn_W2"], 1),
    }
    arrays = {f"in_{k}_dram": _np.ascontiguousarray(v) for k, v in arrays.items()}

    nc = _bacc.Bacc("TRN2", target_bir_lowering=False, num_devices=1)
    args = [nc.dram_tensor(k, v.shape, _mybir.dt.from_np(v.dtype), kind="ExternalInput").ap() for k, v in arrays.items()]
    out = nc.dram_tensor("out_dram", (NTOK, D), _mybir.dt.float32, kind="ExternalOutput").ap()
    moe_gnn(nc, *args, out)
    r = _run(nc, [arrays], core_ids=[0])
    return r.results[0]["out_dram"].reshape(NB, NODES, D)
```
